# Optimizing a Trainium2 kernel written in Bass

```python
import numpy as np
import jax
import jax.numpy as jnp

def _softmax(x, axis=-1):
    return jax.nn.softmax(x, axis=axis)

def _gelu(x):
    return jax.nn.gelu(x, approximate=True)

def _silu(x):
    return jax.nn.silu(x)

def _sigmoid(x):
    return jax.nn.sigmoid(x)

def _layernorm(x, axis=-1, eps=1e-05):
    m = jnp.mean(x, axis=axis, keepdims=True)
    v = jnp.var(x, axis=axis, keepdims=True)
    return (x - m) / jnp.sqrt(v + eps)

def _scatter_add(tgt, idx, src, axis=0):
    return tgt.at[idx].add(src)

def _segment_sum(src, seg, n):
    return jax.ops.segment_sum(src, seg, n)
kernel_name = 'mk_adj_ffn_d1_adj_r2_58db5b'

def setup_inputs(seed: int=0):
    np.random.seed(seed)
    _w = jnp.asarray

    def _rec_inputs():
        import jax
        import jax.numpy as jnp
        _gk = jax.random.key(seed)
        x = 7.22e-05 + 1 * jax.random.normal(jax.random.fold_in(_gk, 1), (16, 512, 256), jnp.float32)
        _w = (1.0 + jnp.arange(512, dtype=jnp.float32)) ** (-0.5)
        _w = _w / _w.mean()
        _pij = jnp.clip(0.00390625 * _w[:, None] * _w[None, :], 0.0, 1.0)
        _a = jax.random.uniform(jax.random.fold_in(_gk, 2), (16, 512, 512)) < _pij
        _a = jnp.logical_or(_a, jnp.swapaxes(_a, -1, -2))
        _a = jnp.logical_or(_a, jnp.eye(512, dtype=bool))
        _af = _a.astype(jnp.float32)
        _af = _af * jax.random.uniform(jax.random.fold_in(_gk, 3), (16, 512, 512), jnp.float32, 0.05, 1)
        adj = _af
        return (x, adj)
    x, adj = _rec_inputs()

    def _L0_gnn_setup():
        import jax, jax.numpy as jnp
        import numpy as np
        EPS_LN = 1e-05

        def hypergraph_conv(x, adj, W, b):
            N, C, _ = adj.shape
            H = (adj != 0).astype(x.dtype)
            w = adj.reshape(N, -1)[:, :C]
            xw = jnp.einsum('ncd,hd->nch', x, W)
            Dn = jnp.einsum('nce,ne->nc', H, w)
            Dn = jnp.where(Dn > 0, 1.0 / Dn, 0.0)
            Be = H.sum(axis=1)
            Be = jnp.where(Be > 0, 1.0 / Be, 0.0)
            m = Be[:, :, None] * jnp.einsum('nce,nch->neh', H, xw)
            out = Dn[:, :, None] * jnp.einsum('nce,neh->nch', H, m)
            return out + b

        def layer_norm(x, g, b):
            mu = jnp.mean(x, axis=-1, keepdims=True)
            var = jnp.var(x, axis=-1, keepdims=True)
            return (x - mu) * jax.lax.rsqrt(var + EPS_LN) * g + b
        key = jax.random.key(seed)
        ks = jax.random.split(key, 4)
        N, C, Din, Dh, Dout = (16, 512, 256, 512, 256)
        x = jax.random.normal(ks[0], (N, C, Din), dtype=jnp.float32)
        adj = jax.random.uniform(ks[1], (N, C, C), dtype=jnp.float32, minval=0.1, maxval=1.0)
        W1 = jax.random.normal(ks[2], (Dh, Din), dtype=jnp.float32) * (1.0 / np.sqrt(Din))
        b1 = jnp.zeros((Dh,), dtype=jnp.float32)
        gamma = jnp.ones((Dh,), dtype=jnp.float32)
        beta = jnp.zeros((Dh,), dtype=jnp.float32)
        W2 = jax.random.normal(ks[3], (Dout, Dh), dtype=jnp.float32) * (1.0 / np.sqrt(Dh))
        b2 = jnp.zeros((Dout,), dtype=jnp.float32)
        return {'x': x, 'adj': adj, 'W1': W1, 'b1': b1, 'gamma': gamma, 'beta': beta, 'W2': W2, 'b2': b2}
    _L0_gnn_all = _L0_gnn_setup()
    _L0_gnn_in = {k: v for k, v in _L0_gnn_all.items() if k in ('W1', 'b1', 'gamma', 'beta', 'W2', 'b2')}
    del _L0_gnn_all

    def _L0_ffn_setup():
        import jax, jax.numpy as jnp
        import numpy as np
        B, S, DIM, E, K = (8, 4096, 256, 4, 2)
        EPS = 1e-06
        key = jax.random.key(seed)
        ks = jax.random.split(key, 4)
        scale = 0.02
        return {'x': jax.random.normal(ks[0], (B, S, DIM), dtype=jnp.float32), 'router_w': jax.random.normal(ks[1], (DIM, E), dtype=jnp.float32) * scale, 'router_b': jnp.zeros((E,), jnp.float32), 'expert_w': jax.random.normal(ks[2], (E, DIM, DIM), dtype=jnp.float32) * scale, 'expert_b': jnp.zeros((E, DIM), jnp.float32), 'out_w': jax.random.normal(ks[3], (DIM, DIM), dtype=jnp.float32) * scale, 'out_b': jnp.zeros((DIM,), jnp.float32), 'norm_w': jnp.ones((DIM,), jnp.float32)}
    _L0_ffn_all = _L0_ffn_setup()
    _L0_ffn_in = {k: v for k, v in _L0_ffn_all.items() if k in ('router_w', 'router_b', 'expert_w', 'expert_b', 'out_w', 'out_b', 'norm_w')}
    del _L0_ffn_all
    return {'x': x, 'adj': adj, 'L0_gnn_W1': _L0_gnn_in['W1'], 'L0_gnn_b1': _L0_gnn_in['b1'], 'L0_gnn_gamma': _L0_gnn_in['gamma'], 'L0_gnn_beta': _L0_gnn_in['beta'], 'L0_gnn_W2': _L0_gnn_in['W2'], 'L0_gnn_b2': _L0_gnn_in['b2'], 'L0_ffn_router_w': _L0_ffn_in['router_w'], 'L0_ffn_router_b': _L0_ffn_in['router_b'], 'L0_ffn_expert_w': _L0_ffn_in['expert_w'], 'L0_ffn_expert_b': _L0_ffn_in['expert_b'], 'L0_ffn_out_w': _L0_ffn_in['out_w'], 'L0_ffn_out_b': _L0_ffn_in['out_b'], 'L0_ffn_norm_w': _L0_ffn_in['norm_w']}

def reference(x, adj, L0_gnn_W1, L0_gnn_b1, L0_gnn_gamma, L0_gnn_beta, L0_gnn_W2, L0_gnn_b2, L0_ffn_router_w, L0_ffn_router_b, L0_ffn_expert_w, L0_ffn_expert_b, L0_ffn_out_w, L0_ffn_out_b, L0_ffn_norm_w):
    import jax
    import jax.numpy as jnp

    def _L0_gnn_ref(x, adj, W1, b1, gamma, beta, W2, b2):
        import jax, jax.numpy as jnp
        import numpy as np
        EPS_LN = 1e-05

        def hypergraph_conv(x, adj, W, b):
            N, C, _ = adj.shape
            H = (adj != 0).astype(x.dtype)
            w = adj.reshape(N, -1)[:, :C]
            xw = jnp.einsum('ncd,hd->nch', x, W)
            Dn = jnp.einsum('nce,ne->nc', H, w)
            Dn = jnp.where(Dn > 0, 1.0 / Dn, 0.0)
            Be = H.sum(axis=1)
            Be = jnp.where(Be > 0, 1.0 / Be, 0.0)
            m = Be[:, :, None] * jnp.einsum('nce,nch->neh', H, xw)
            out = Dn[:, :, None] * jnp.einsum('nce,neh->nch', H, m)
            return out + b

        def layer_norm(x, g, b):
            mu = jnp.mean(x, axis=-1, keepdims=True)
            var = jnp.var(x, axis=-1, keepdims=True)
            return (x - mu) * jax.lax.rsqrt(var + EPS_LN) * g + b
        h = jax.nn.relu(hypergraph_conv(x, adj, W1, b1))
        h = layer_norm(h, gamma, beta)
        y = hypergraph_conv(h, adj, W2, b2)
        return y + x

    def _L0_ffn_ref(x, router_w, router_b, expert_w, expert_b, out_w, out_b, norm_w):
        import jax, jax.numpy as jnp
        import numpy as np
        B, S, DIM, E, K = (8, 4096, 256, 4, 2)
        EPS = 1e-06
        b, s, d = x.shape
        logits = x @ router_w + router_b
        topw, topi = jax.lax.top_k(logits, K)
        topw = jax.nn.softmax(topw, axis=-1)
        t = b * s
        xf = x.reshape(t, d)
        idx = topi.reshape(t, K)
        w = topw.reshape(t, K).astype(x.dtype)
        mask = jnp.zeros((t, E), x.dtype).at[jnp.arange(t)[:, None], idx].set(w)
        h = jax.nn.silu(jnp.einsum('td,edh->teh', xf, expert_w) + expert_b)
        comb = jnp.einsum('te,teh->th', mask, h)
        out = comb @ out_w + out_b
        y = xf + out
        rms = jnp.sqrt(jnp.mean(y * y, axis=-1, keepdims=True) + EPS)
        return (norm_w * (y / rms)).reshape(b, s, d)
    x = x + _L0_gnn_ref(_layernorm(x, axis=-1), adj, L0_gnn_W1, L0_gnn_b1, L0_gnn_gamma, L0_gnn_beta, L0_gnn_W2, L0_gnn_b2)
    x = x + _L0_ffn_ref(_layernorm(x, axis=-1), L0_ffn_router_w, L0_ffn_router_b, L0_ffn_expert_w, L0_ffn_expert_b, L0_ffn_out_w, L0_ffn_out_b, L0_ffn_norm_w)
    return x

_drawn_inputs = setup_inputs


def setup_inputs(seed=0):
    import zlib

    import numpy as np

    out = dict(_drawn_inputs(seed))
    spreads = {'L0_gnn_b1': (0.0, 0.1),
     'L0_gnn_gamma': (1.0, 0.2),
     'L0_gnn_beta': (0.0, 0.1),
     'L0_gnn_b2': (0.0, 0.474),
     'L0_ffn_router_b': (0.0, 2.0),
     'L0_ffn_expert_b': (0.0, 0.8),
     'L0_ffn_out_b': (0.0, 1.81),
     'L0_ffn_norm_w': (1.0, 0.6)}
    factors = {'L0_ffn_router_w': 8.0, 'L0_ffn_expert_w': 8.0, 'L0_ffn_out_w': 8.0}
    for name, (base, spread) in spreads.items():
        noise = np.random.default_rng([zlib.crc32(name.encode()), seed]).standard_normal(out[name].shape)
        drawn = base * np.exp(spread * noise) if base else spread * noise
        out[name] = jnp.asarray(drawn.astype(out[name].dtype))
    for name, factor in factors.items():
        out[name] = (out[name] * factor).astype(out[name].dtype)
    return out
```

```python
from contextlib import ExitStack

import concourse.bass as bass
from concourse import mybir

ALU = mybir.AluOpType
ACT = mybir.ActivationFunctionType
F32 = mybir.dt.float32
F16 = mybir.dt.float16
BF16 = mybir.dt.bfloat16
I32 = mybir.dt.int32
X = mybir.AxisListType.X
RMAX = bass.bass_isa.ReduceOp.max

P = 128
EPS_LN = 1e-5
EPS_RMS = 1e-6

XS = 2.0 ** 11
A2S = 2.0 ** -9
HS = 2.0 ** 10
WS = 2.0 ** 13
VS = 2.0 ** -19


def build(nc, x, adj, wrow, w1t, b1, gamma, beta, w2t, b2, rw, rb, ew, eb, ow, ob, nw, out):
    N, C, D = x.shape
    DH = w1t.shape[1]
    NE = ew.shape[1]
    CT, KD, KH = C // P, D // P, DH // P
    CG = 2
    assert (C, D, DH, NE) == (512, 256, 512, 4)

    with ExitStack() as ctx:
        def sb(name, shape, dt):
            return ctx.enter_context(nc.sbuf_tensor(name, shape, dt))

        def sem(name):
            return ctx.enter_context(nc.semaphore(name))

        bank = [ctx.enter_context(nc.psum_tensor(f"bank{i}", [P, 512], F32)) for i in range(8)]
        HT_BANK, A1_BANK, D_BANK, A2_BANK = (0, 2, 3, 1), (0, 2), 4, (3, 1)
        A3_BANK, HNT_BANK, V_BANK, U_BANK, B3_BANK = (0, 2, 3, 1), (4, 0, 4, 0), (1, 2), (3, 4), (1, 4)
        XT_BANK, R_BANK, E_BANK, CT_BANK, O_BANK = (5, 6), 7, (5, 6, 7, 5, 6, 7, 5, 6), (7, 5), (6, 7)

        w1f = sb("w1f", [P, KD, DH], F32)
        w2f = sb("w2f", [P, KH, D], F32)
        w2g = sb("w2g", [P, KH, D], F32)
        ewf = sb("ewf", [P, KD, NE * D], F32)
        owf = sb("owf", [P, KD, D], F32)
        rwf = sb("rwf", [P, KD, NE], F32)
        w1h, w1l = sb("w1h", [P, KD, DH], F16), sb("w1l", [P, KD, DH], F16)
        w2h, w2l = sb("w2h", [P, KH, D], F16), sb("w2l", [P, KH, D], F16)
        ewh, ewl = sb("ewh", [P, KD, NE * D], F16), sb("ewl", [P, KD, NE * D], F16)
        owh, owl = sb("owh", [P, KD, D], F16), sb("owl", [P, KD, D], F16)
        rwh, rwl = sb("rwh", [P, KD, NE], F16), sb("rwl", [P, KD, NE], F16)
        gam, bet = sb("gam", [P, KH], F32), sb("bet", [P, KH], F32)
        b1b = sb("b1b", [P, DH], F32)
        b2b = sb("b2b", [P, CT, D], F32)
        obb = sb("obb", [P, CT, D], F32)
        nwb = sb("nwb", [P, D], F32)
        rbb = sb("rbb", [P, CT, NE], F32)
        ebrow = sb("ebrow", [1, NE * D], F32)
        brow = sb("brow", [1, NE * D], F32)
        bwrow = sb("bwrow", [1, D], F32)
        ebias = sb("ebias", [P, NE * D], BF16)
        vbias = sb("vbias", [P, D], BF16)
        ones = sb("ones", [P, P], BF16)
        absbuf = sb("absbuf", [P, 2048], F32)
        mags = sb("mags", [P, 8], F32)
        pmax = sb("pmax", [P, 8], F32)
        pw = sb("pw", [P, 8], F32)
        ipw = sb("ipw", [P, 8], F32)
        wsc = sb("wsc", [P, 8], F32)
        ksc = sb("ksc", [P, 8], F32)
        ident = sb("ident", [P, P], F32)
        ident16 = sb("ident16", [P, P], F16)
        epsln, epsrms = sb("epsln", [P, CT], F32), sb("epsrms", [P, CT], F32)
        mhalf, mone = sb("mhalf", [P, CT], F32), sb("mone", [P, CT], F32)
        invd = sb("invd", [P, CT], F32)
        tri = sb("tri", [P, CT, NE, NE], F32)
        wf = sb("wf", [P, N, CT], F32)
        wr1, wr2 = sb("wr1", [P, N, CT], F32), sb("wr2", [P, N, CT], F32)
        wparts = sb("wparts", [P, N, CT, 3], BF16)

        xin = sb("xin", [P, CT, D], F32)
        adjin = sb("adjin", [P, CT, C], F32)
        h16 = sb("h16", [P, CT, C], F16)
        ht16 = sb("ht16", [P, CT, C], F16)
        wcur = sb("wcur", [P, CT, 3], BF16)
        xbn = sb("xbn", [P, CT, 6], F32)
        xmv = sb("xmv", [P, CT, 2], F32)
        xve, xrs, xnm, xnb = (sb(n, [P, CT], F32) for n in ("xve", "xrs", "xnm", "xnb"))
        xn = sb("xn", [P, CT, D], F32)
        xsh, xsl = sb("xsh", [P, CT, D], F16), sb("xsl", [P, CT, D], F16)
        xb = sb("xb", [P, CT, D], F32)
        deg, dmax, be = (sb(n, [P, CT], F32) for n in ("deg", "dmax", "be"))
        dsum, dclip, drec, dn, dna, dnb = (sb(n, [P, CT], F32) for n in ("dsum", "dclip", "drec", "dn", "dna", "dnb"))
        a1h, a1l = sb("a1h", [P, CT, D], F16), sb("a1l", [P, CT, D], F16)
        a2h, a2l = sb("a2h", [P, KD, C], F16), sb("a2l", [P, KD, C], F16)
        z = sb("z", [P, CT, DH], F32)
        r = sb("r", [P, CT, DH], F32)
        hbn = sb("hbn", [P, CT, 6], F32)
        hmv = sb("hmv", [P, CT, 2], F32)
        hve, hrs, hnm, hnb = (sb(n, [P, CT], F32) for n in ("hve", "hrs", "hnm", "hnb"))
        hn = sb("hn", [P, CT, DH], F32)
        hnth, hntl = sb("hnth", [P, CT, KH * P], F16), sb("hntl", [P, CT, KH * P], F16)
        vh, vl = sb("vh", [P, CT, D], F16), sb("vl", [P, CT, D], F16)
        uh, ul = sb("uh", [P, CT, D], F16), sb("ul", [P, CT, D], F16)
        x1 = sb("x1", [P, CT, D], F32)
        ybn = sb("ybn", [P, CT, 6], F32)
        ymv = sb("ymv", [P, CT, 2], F32)
        yve, yrs, ynm, ynb = (sb(n, [P, CT], F32) for n in ("yve", "yrs", "ynm", "ynb"))

        x1k = sb("x1k", [P, CT, D], F32)
        x2 = sb("x2", [P, CT, D], F32)
        x2o = sb("x2o", [P, CT, D], F32)
        xth, xtl = sb("xth", [P, KD, C], F16), sb("xtl", [P, KD, C], F16)
        spare = sb("spare", [P, 1], F32)
        lg = sb("lg", [P, CT, NE], F32)
        ldf, tie, beat = (sb(n, [P, CT, NE, NE], F32) for n in ("ldf", "tie", "beat"))
        rank, lsel, arg, th, wt, mask = (sb(n, [P, CT, NE], F32) for n in ("rank", "lsel", "arg", "th", "wt", "mask"))
        lsum = sb("lsum", [P, CT], F32)
        silu = sb("silu", [P, 4, 512], F32)
        comb = sb("comb", [P, CT, D], F32)
        cth, ctl = sb("cth", [P, KD, C], F16), sb("ctl", [P, KD, C], F16)
        y = sb("y", [P, CT, D], F32)
        ysq = sb("ysq", [P, D], F32)
        yss, yms, yme, yrr = (sb(n, [P, CT], F32) for n in ("yss", "yms", "yme", "yrr"))
        yf = sb("yf", [P, CT, D], F32)
        outb = sb("outb", [P, CT, D], F32)

        w_in, c_pool, c_dve, c_act, c_pe = (sem(n) for n in ("w_in", "c_pool", "c_dve", "c_act", "c_pe"))

        x_in, adj_in, out_st = sem("x_in"), sem("adj_in"), sem("out_st")
        ht_rdy, a3_rdy, hnt_rdy = sem("ht_rdy"), sem("a3_rdy"), sem("hnt_rdy")
        a1_rdy, a2_rdy, v_rdy, u_rdy, b3_rdy = (sem(n) for n in ("a1_rdy", "a2_rdy", "v_rdy", "u_rdy", "b3_rdy"))
        xt_rdy, ct_rdy, o_rdy = sem("xt_rdy"), sem("ct_rdy"), sem("o_rdy")
        d_rdy, lg_rdy = sem("d_rdy"), sem("lg_rdy")
        e_rdy = sem("e_rdy")
        ht_cp, a1_hi, relu_dn, hn_dn, hnt_hi, u_hi, x2_dn, sq_dn, xn_dn = (
            sem(n) for n in ("ht_cp", "a1_hi", "relu_dn", "hn_dn", "hnt_hi", "u_hi", "x2_dn", "sq_dn", "xn_dn"))
        a2_hi, v_hi, xt_hi, ct_hi = (sem(n) for n in ("a2_hi", "v_hi", "xt_hi", "ct_hi"))
        xs_hi, th_dn = sem("xs_hi"), sem("th_dn")
        silu_dn = sem("silu_dn")
        h_made, be_max, be_dn, xs_lo, xstat, lg_dn, arg_dn, mask_dn = (
            sem(n) for n in ("h_made", "be_max", "be_dn", "xs_lo", "xstat", "lg_dn", "arg_dn", "mask_dn"))
        d_step = sem("d_step")
        r_step = sem("r_step")
        a1_lo, z_dn, hbn_dn, hstat, hnt_lo, u_lo, x1_dn, ybn_dn, xbn_dn, yf_dn = (
            sem(n) for n in ("a1_lo", "z_dn", "hbn_dn", "hstat", "hnt_lo", "u_lo", "x1_dn", "ybn_dn", "xbn_dn", "yf_dn"))
        ystat = sem("ystat")
        a2_lo, v_lo, xt_lo, ct_lo, y_dn = (sem(n) for n in ("a2_lo", "v_lo", "xt_lo", "ct_lo", "y_dn"))
        comb_st = sem("comb_st")
        xrs_st, yrs_st = sem("xrs_st"), sem("yrs_st")
        hrs_st = sem("hrs_st")
        rr_st = sem("rr_st")
        xb_st = sem("xb_st")
        w_cur, x1_kept, x2o_dn = sem("w_cur"), sem("x1_kept"), sem("x2o_dn")
        out_rdy = sem("out_rdy")

        def steps(eng, body, prep):
            body(eng, 0, True, False, True)
            with eng.Fori(1, N - 1) as g:
                body(eng, g, True, True, True)
            body(eng, N - 1, True, True, False)
            body(eng, N, False, True, False)

        block = ctx.enter_context(nc.Block())

        NWEIGHTS = 14


        @block.sync
        def _(sp):
            sp.dma_start(xin[:, :, :], x[0].rearrange("(t p) d -> p t d", p=P)).then_inc(x_in, 16)
            sp.dma_start(adjin[:, :, :], adj[0].rearrange("(t p) e -> p t e", p=P)).then_inc(adj_in, 16)
            for dst, src in (
                (w2f[:, :, :], w2t.rearrange("(k p) f -> p k f", p=P)),
                (gam[:, :], gamma), (bet[:, :], beta),
                (w1f[:, :, :], w1t.rearrange("(k p) h -> p k h", p=P)),
                (ewf[:, :, :].rearrange("p k (e h) -> p k e h", e=NE), ew.rearrange("(k p) e h -> p k e h", p=P)),
                (owf[:, :, :], ow.rearrange("(k p) h -> p k h", p=P)),
                (rwf[:, :, :], rw.rearrange("(k p) e -> p k e", p=P)),
                (ebrow[:, :], eb), (wf[:, :, :], wrow),
                (b1b[:, :], b1.to_broadcast([P, DH])),
                (b2b[:, 0, :], b2.to_broadcast([P, D])), (obb[:, 0, :], ob.to_broadcast([P, D])),
                (nwb[:, :], nw.to_broadcast([P, D])), (rbb[:, 0, :], rb.to_broadcast([P, NE])),
            ):
                sp.dma_start(dst, src).then_inc(w_in, 16)

            def body(sp, g, conv, ffn, prep):
                if prep:
                    sp.wait_ge(h_made, g + 1)
                    sp.dma_start(adjin[:, :, :], adj[g + 1].rearrange("(t p) e -> p t e", p=P)).then_inc(adj_in, 16)
                    sp.wait_ge(xb_st, 2 * g + 2)
                    sp.dma_start(xin[:, :, :], x[g + 1].rearrange("(t p) d -> p t d", p=P)).then_inc(x_in, 16)
                if ffn:
                    f = g - 1
                    for j in range(2):
                        sp.wait_ge(out_rdy, 2 * f + j + 1)
                        sp.dma_start(out[f].rearrange("(t p) d -> p t d", p=P)[:, CG * j:CG * j + CG, :],
                                     outb[:, CG * j:CG * j + CG, :]).then_inc(out_st, 16)
            steps(sp, body, None)
            sp.wait_ge(out_st, 32 * N)

        @block.gpsimd
        def _(gp):
            tt = nc.gpsimd.tensor_tensor
            nc.gpsimd.memset(ident[:, :], 0.0).then_inc(c_pool, 1)
            nc.gpsimd.memset(ident16[:, :], 0.0).then_inc(c_pool, 1)
            nc.gpsimd.memset(tri[:, :, :, :], 1.0).then_inc(c_pool, 1)
            for t, v in ((epsln, EPS_LN), (epsrms, EPS_RMS), (mhalf, -0.5), (mone, -1.0), (invd, 1.0 / D)):
                nc.gpsimd.memset(t[:, :], v).then_inc(c_pool, 1)
            gp.wait_ge(c_pool, 8)
            for m in (ident, ident16):
                gp.affine_select(out=m[:, :], in_=m[:, :], compare_op=ALU.not_equal, fill=1.0, base=0,
                                 pattern=[[-1, P]], channel_multiplier=1).then_inc(c_pool, 1)
            gp.affine_select(out=tri[:, :, :, :], in_=tri[:, :, :, :], compare_op=ALU.is_gt, fill=0.0, base=0,
                             pattern=[[0, CT], [1, NE], [-1, NE]], channel_multiplier=0).then_inc(c_pool, 1)

            def root(stat, mv, ve, rs, nm, nb, sem_st, g, per, k, s, stat_per, stat_k):
                gp.wait_ge(stat, stat_per * g + stat_k)
                tt(ve[:, s], mv[:, s, 1], epsln[:, s], ALU.add).then_inc(sem_st, 1)
                tt(nm[:, s], mv[:, s, 0], mone[:, s], ALU.mult).then_inc(sem_st, 1)
                gp.wait_ge(sem_st, per * g + k + 2)
                tt(rs[:, s], ve[:, s], mhalf[:, s], ALU.pow).then_inc(sem_st, 1)
                gp.wait_ge(sem_st, per * g + k + 3)
                tt(nb[:, s], nm[:, s], rs[:, s], ALU.mult).then_inc(sem_st, 1)

            ALL = slice(0, CT)

            def prep_x(g, again=True):
                if again:
                    gp.wait_ge(d_rdy, g)
                root(xstat, xmv, xve, xrs, xnm, xnb, xrs_st, g, 4, 0, ALL, 1, 1)
                nc.gpsimd.tensor_copy(wcur[:, :, :], wparts[:, g, :, :]).then_inc(w_cur, 1)

            def make_xb(g, again=True):
                gp.wait_ge(xn_dn, 4 * g + 4)
                if again:
                    gp.wait_ge(x1_dn, 4 * g)
                tt(xb[:, :, :], xin[:, :, :], xn[:, :, :], ALU.add).then_inc(xb_st, 1)
                gp.wait_ge(xb_st, 2 * g + 1)
                tt(xb[:, :, :], xb[:, :, :], b2b[:, :, :], ALU.add).then_inc(xb_st, 1)

            gp.wait_ge(c_dve, 1)
            nc.gpsimd.partition_all_reduce(pmax[:, :], mags[:, :], P, RMAX).then_inc(c_pool, 1)
            gp.wait_ge(c_dve, 2)
            prep_x(0, again=False)
            make_xb(0, again=False)

            def body(gp, g, conv, ffn, prep):
                f = g - 1
                if ffn:
                    gp.wait_ge(x2_dn, 4 * f + 4)
                    if not prep:
                        gp.wait_ge(out_rdy, 2 * f)
                    tt(x2o[:, :, :], x2[:, :, :], obb[:, :, :], ALU.add).then_inc(x2o_dn, 1)
                    nc.gpsimd.tensor_copy(x1k[:, :, :], x1[:, :, :]).then_inc(x1_kept, 1)
                if prep:
                    prep_x(g + 1)
                if conv:
                    for t in range(CT):
                        root(hstat, hmv, hve, hrs, hnm, hnb, hrs_st, g, 16, 4 * t, slice(t, t + 1), 4, t + 1)
                if ffn:
                    gp.wait_ge(sq_dn, 4 * f + 4)
                    tt(yms[:, :], yss[:, :], invd[:, :], ALU.mult).then_inc(rr_st, 1)
                    gp.wait_ge(rr_st, 3 * f + 1)
                    tt(yme[:, :], yms[:, :], epsrms[:, :], ALU.add).then_inc(rr_st, 1)
                    gp.wait_ge(rr_st, 3 * f + 2)
                    tt(yrr[:, :], yme[:, :], mhalf[:, :], ALU.pow).then_inc(rr_st, 1)
                if conv:
                    root(ystat, ymv, yve, yrs, ynm, ynb, yrs_st, g, 4, 0, ALL, 1, 1)
                if ffn:
                    for j in range(2):
                        s = slice(CG * j, CG * j + CG)
                        gp.wait_ge(yf_dn, 4 * f + CG * j + CG)
                        tt(outb[:, s, :], yf[:, s, :], x1k[:, s, :], ALU.add).then_inc(out_rdy, 1)
                if prep:
                    make_xb(g + 1)
                if ffn:
                    gp.wait_ge(out_st, 32 * f + 32)
            steps(gp, body, None)

        @block.scalar
        def _(act):
            af = nc.scalar.activation

            def prep_x(g, again=True):
                act.wait_ge(xrs_st, 4 * g + 4)
                if again:
                    act.wait_ge(xb_st, 2 * g)
                    act.wait_ge(xs_lo, g)
                for t in range(CT):
                    af(xn[:, t, :], xin[:, t, :], ACT.Identity, bias=xnb[:, t:t + 1],
                       scale=xrs[:, t:t + 1]).then_inc(xn_dn, 1)
                act.wait_ge(xn_dn, 4 * g + 4)
                if again:
                    act.wait_ge(a1_rdy, 2 * g)
                af(xsh[:, :, :], xn[:, :, :], ACT.Copy, scale=XS).then_inc(xs_hi, 1)

            act.wait_ge(c_pool, 8)
            af(ysq[:, 0:1], epsln[:, 0:1], ACT.Silu).then_inc(c_act, 1)
            prep_x(0, again=False)
            act.wait_ge(c_dve, 3)
            for i, (full, hi) in enumerate(((w1f, w1h), (w2g, w2h), (ewf, ewh), (owf, owh), (rwf, rwh))):
                af(hi[:, :, :], full[:, :, :], ACT.Copy, scale=wsc[:, i:i + 1]).then_inc(c_act, 1)

            def hi_rows(dst, src, t, scale, s_hi):
                af(dst, src, ACT.Copy, scale=scale).then_inc(s_hi, 1)

            def expert(act, f, i):
                act.wait_ge(e_rdy, 8 * f + i + 1)
                if i >= 4:
                    act.wait_ge(comb_st, 16 * f + 4 * ((i - 4) // 2) + 4)
                af(silu[:, i % 4, :], bank[E_BANK[i]][:, :], ACT.Silu, scale=ksc[:, 2:3]).then_inc(silu_dn, 1)

            def relu(act, g, t):
                act.wait_ge(z_dn, 4 * g + t + 1)
                af(r[:, t, :], z[:, t, :], ACT.Relu).then_inc(relu_dn, 1)

            def norm_h(act, g, t):
                act.wait_ge(hrs_st, 16 * g + 4 * t + 4)
                af(hn[:, t, :], r[:, t, :], ACT.Identity, bias=hnb[:, t:t + 1],
                   scale=hrs[:, t:t + 1]).then_inc(hn_dn, 1)

            def hnt_part(act, g, t):
                act.wait_ge(hnt_rdy, 4 * g + t + 1)
                af(hnth[:, t, :], bank[HNT_BANK[t]][:, :], ACT.Copy, scale=HS).then_inc(hnt_hi, 1)

            def v_part(act, g, j):
                act.wait_ge(v_rdy, 2 * g + j + 1)
                af(vh[:, CG * j:CG * j + CG, :], bank[V_BANK[j]][:, :].rearrange("p (t d) -> p t d", t=CG),
                   ACT.Copy, scale=VS).then_inc(v_hi, 1)

            def ct_part(act, f, j):
                act.wait_ge(ct_rdy, 2 * f + j + 1)
                af(cth[:, :, 256 * j:256 * j + 256], bank[CT_BANK[j]][:, :].rearrange("p (k c) -> p k c", k=KD),
                   ACT.Copy).then_inc(ct_hi, 1)

            def squares(act, f, j):
                act.wait_ge(y_dn, 2 * f + j + 1)
                for t in range(CG * j, CG * j + CG):
                    if t > 0:
                        act.wait_ge(sq_dn, 4 * f + t)
                    af(ysq[:, :], y[:, t, :], ACT.Square, accum_out=yss[:, t:t + 1]).then_inc(sq_dn, 1)

            def body(act, g, conv, ffn, prep):
                f = g - 1
                if conv:
                    if ffn:
                        act.wait_ge(be_max, g)
                    for k in range(CT):
                        act.wait_ge(ht_rdy, 4 * g + k + 1)
                        af(ht16[:, k, :], bank[HT_BANK[k]][:, 0:256].bitcast(F16), ACT.Copy,
                           accum_out=deg[:, k:k + 1]).then_inc(ht_cp, 1)
                if ffn:
                    act.wait_ge(yrs_st, 4 * f + 4)
                    for t in range(CT):
                        af(x2[:, t, :], x1[:, t, :], ACT.Identity, bias=ynb[:, t:t + 1],
                           scale=yrs[:, t:t + 1]).then_inc(x2_dn, 1)
                if conv:
                    act.wait_ge(be_dn, g + 1)
                    for e in range(CT):
                        if e % CG == 0:
                            act.wait_ge(a1_rdy, 2 * g + e // CG + 1)
                        af(a1h[:, e, :], bank[A1_BANK[e // CG]][:, 256 * (e % CG):256 * (e % CG) + 256], ACT.Copy,
                           scale=be[:, e:e + 1]).then_inc(a1_hi, 1)
                if ffn:
                    for j in range(2):
                        act.wait_ge(xt_rdy, 2 * f + j + 1)
                        af(xth[:, :, 256 * j:256 * j + 256],
                           bank[XT_BANK[j]][:, :].rearrange("p (k c) -> p k c", k=KD),
                           ACT.Copy, scale=XS).then_inc(xt_hi, 1)
                if conv:
                    for k in range(KD):
                        act.wait_ge(a2_rdy, 2 * g + k + 1)
                        af(a2h[:, k, :], bank[A2_BANK[k]][:, :], ACT.Copy, scale=A2S).then_inc(a2_hi, 1)
                if ffn:
                    act.wait_ge(arg_dn, f + 1)
                    af(th[:, :, :], arg[:, :, :], ACT.Tanh).then_inc(th_dn, 1)
                    expert(act, f, 0)
                    expert(act, f, 1)
                if prep:
                    prep_x(g + 1)
                if conv:
                    relu(act, g, 0)
                    relu(act, g, 1)
                    relu(act, g, 2)
                    norm_h(act, g, 0)
                    relu(act, g, 3)
                    norm_h(act, g, 1)
                if ffn:
                    expert(act, f, 2)
                if conv:
                    norm_h(act, g, 2)
                if ffn:
                    expert(act, f, 3)
                if conv:
                    norm_h(act, g, 3)
                if ffn:
                    for i in range(4, 8):
                        expert(act, f, i)
                if conv:
                    hnt_part(act, g, 0)
                    hnt_part(act, g, 1)
                    hnt_part(act, g, 2)
                    v_part(act, g, 0)
                    hnt_part(act, g, 3)
                if ffn:
                    ct_part(act, f, 0)
                if conv:
                    v_part(act, g, 1)
                if ffn:
                    ct_part(act, f, 1)
                    squares(act, f, 0)
                if conv:
                    for e in range(CT):
                        if e % CG == 0:
                            act.wait_ge(u_rdy, 2 * g + e // CG + 1)
                        af(uh[:, e, :], bank[U_BANK[e // CG]][:, 256 * (e % CG):256 * (e % CG) + 256], ACT.Copy,
                           scale=be[:, e:e + 1]).then_inc(u_hi, 1)
                if ffn:
                    squares(act, f, 1)
            steps(act, body, None)

        @block.vector
        def _(dve):
            v = nc.vector
            TT, TS, STT = v.tensor_tensor, v.tensor_scalar, v.scalar_tensor_tensor
            own = sem("dve_setup")
            count = [0]

            def done(ins):
                count[0] += 1
                ins.then_inc(own, 1)
                dve.wait_ge(own, count[0])

            def prep_h(g, again=True):
                dve.wait_ge(adj_in, 16 * g + 16)
                if again:
                    dve.wait_ge(u_rdy, 2 * g)
                TS(h16[:, :, :], adjin[:, :, :], 0.0, None, ALU.not_equal).then_inc(h_made, 1)

            def prep_x_stats(g):
                dve.wait_ge(x_in, 16 * g + 16)
                for t in range(CT):
                    v.bn_stats(xbn[:, t, :], xin[:, t, :]).then_inc(xbn_dn, 1)

            def prep_x_aggr(g, again=True):
                dve.wait_ge(xbn_dn, 4 * g + 4)
                if again:
                    dve.wait_ge(xrs_st, 4 * g)
                v.memset(spare[:, :], 0.0)
                for t in range(CT):
                    ins = v.bn_aggr(xmv[:, t, :], xbn[:, t, :])
                ins.then_inc(xstat, 1)

            def prep_x_lo(g):
                dve.wait_ge(xs_hi, g + 1)
                STT(xsl[:, :, :], xn[:, :, :], XS, xsh[:, :, :], ALU.mult, ALU.subtract).then_inc(xs_lo, 1)

            prep_h(0, again=False)
            prep_x_stats(0)
            prep_x_aggr(0, again=False)
            done(v.memset(mags[:, :], 0.0))
            done(v.memset(ones[:, :], 1.0))
            done(v.memset(ebias[:, :], 0.0))
            done(v.memset(vbias[:, :], 0.0))
            dve.wait_ge(w_in, 16 * NWEIGHTS)
            for k in range(KH):
                done(TS(w2g[:, k, :], w2f[:, k, :], gam[:, k:k + 1], None, ALU.mult))
            for dst in (b2b, obb, rbb):
                for t in range(1, CT):
                    done(v.tensor_copy(dst[:, t, :], dst[:, 0, :]))

            def magnitude(col, src, rows, n, scale):
                done(STT(absbuf[0:rows, 0:n], src, -1.0, src, ALU.mult, ALU.max))
                done(v.reduce_max(mags[0:rows, col:col + 1], absbuf[0:rows, 0:n], X))
                if scale != 1.0:
                    done(TS(mags[0:rows, col:col + 1], mags[0:rows, col:col + 1], scale, None, ALU.mult))

            magnitude(0, w1f[:, :, :].rearrange("p k n -> p (k n)"), P, KD * DH, 1.0)
            magnitude(1, w2g[:, :, :].rearrange("p k n -> p (k n)"), P, KH * D, 1.0)
            magnitude(2, ewf[:, :, :].rearrange("p k n -> p (k n)"), P, KD * NE * D, 1.0)
            magnitude(3, owf[:, :, :].rearrange("p k n -> p (k n)"), P, KD * D, 1.0)
            magnitude(4, rwf[:, :, :].rearrange("p k n -> p (k n)"), P, KD * NE, 1.0)
            magnitude(5, ebrow[0:1, :], 1, NE * D, 1.0 / D)
            dve.wait_ge(c_pe, 1)
            done(v.tensor_copy(bwrow[0:1, :], bank[0][0:1, 0:D]))
            magnitude(6, bwrow[0:1, :], 1, D, 1.0 / DH)
            v.memset(mags[:, 7:8], 0.0).then_inc(c_dve, 1)
            done(v.tensor_copy(wparts[:, :, :, 0], wf[:, :, :]))
            done(TT(wr1[:, :, :], wf[:, :, :], wparts[:, :, :, 0], ALU.subtract))
            done(v.tensor_copy(wparts[:, :, :, 1], wr1[:, :, :]))
            done(TT(wr2[:, :, :], wr1[:, :, :], wparts[:, :, :, 1], ALU.subtract))
            v.tensor_copy(wparts[:, :, :, 2], wr2[:, :, :]).then_inc(c_dve, 1)
            dve.wait_ge(c_pool, 12)
            done(TT(pmax[:, 1:2], pmax[:, 1:2], pmax[:, 6:7], ALU.max))
            done(TT(pmax[:, 2:3], pmax[:, 2:3], pmax[:, 5:6], ALU.max))
            done(TS(pmax[:, :], pmax[:, :], 1e-30, 1e30, ALU.max, ALU.min))
            done(TS(pw[:, :].bitcast(I32), pmax[:, :].bitcast(I32), 0x7F800000, None, ALU.bitwise_and))
            done(v.reciprocal(ipw[:, :], pw[:, :]))
            done(TS(wsc[:, :], ipw[:, :], WS, None, ALU.mult))
            done(TS(ksc[:, 0:1], pw[:, 0:1], 1.0 / (XS * A2S * WS), None, ALU.mult))
            done(TS(ksc[:, 1:2], pw[:, 1:2], 1.0 / (HS * WS * VS), None, ALU.mult))
            done(TS(ksc[:, 2:3], pw[:, 2:3], 1.0 / (XS * WS), None, ALU.mult))
            done(TS(ksc[:, 3:4], pw[:, 3:4], 2.0 ** -5 / WS, pw[:, 2:3], ALU.mult, ALU.mult))
            done(TS(ksc[:, 4:5], pw[:, 4:5], 1.0 / (XS * WS), None, ALU.mult))
            done(TS(ksc[:, 5:6], ipw[:, 2:3], 2.0 ** 4, None, ALU.mult))
            v.tensor_copy(ksc[:, 6:7], ksc[:, 5:6]).then_inc(c_dve, 1)
            for col, n, src, scale, dst in ((1, D, bwrow, HS, vbias), (2, NE * D, ebrow, XS, ebias)):
                done(TS(brow[0:1, 0:n], src[0:1, 0:n], wsc[0:1, col:col + 1], scale, ALU.mult, ALU.mult))
                for part in range(3):
                    row = dst[32 * part:32 * part + 1, 0:n]
                    done(v.tensor_copy(row, brow[0:1, 0:n]))
                    if part < 2:
                        done(v.tensor_copy(absbuf[0:1, 0:n], row))
                        done(TT(brow[0:1, 0:n], brow[0:1, 0:n], absbuf[0:1, 0:n], ALU.subtract))
            dve.wait_ge(c_act, 6)
            for i, (full, hi, lo) in enumerate(((w1f, w1h, w1l), (w2g, w2h, w2l), (ewf, ewh, ewl),
                                                (owf, owh, owl), (rwf, rwh, rwl))):
                ins = STT(lo[:, :, :], full[:, :, :], wsc[:, i:i + 1], hi[:, :, :], ALU.mult, ALU.subtract)
                if i < 4:
                    done(ins)
            ins.then_inc(c_dve, 1)
            prep_x_lo(0)

            def combine(f, t):
                for e in range(NE):
                    src = silu[:, (2 * t + e // 2) % 4, D * (e % 2):D * (e % 2) + D]
                    m = mask[:, t, e:e + 1]
                    if e % 2 == 0:
                        dve.wait_ge(silu_dn, 8 * f + 2 * t + e // 2 + 1)
                    if e == 0:
                        TS(comb[:, t, :], src, m, None, ALU.mult).then_inc(comb_st, 1)
                    else:
                        dve.wait_ge(comb_st, 16 * f + 4 * t + e)
                        STT(comb[:, t, :], src, m, comb[:, t, :], ALU.mult, ALU.add).then_inc(comb_st, 1)

            def z_part(g, t):
                dve.wait_ge(a3_rdy, 4 * g + t + 1)
                STT(z[:, t, :], bank[A3_BANK[t]][:, :], dna[:, t:t + 1], b1b[:, :], ALU.mult, ALU.add).then_inc(z_dn, 1)

            def h_stats(g, t):
                dve.wait_ge(relu_dn, 4 * g + t + 1)
                v.bn_stats(hbn[:, t, :], r[:, t, :]).then_inc(hbn_dn, 1)

            def h_aggr(g, t):
                v.bn_aggr(hmv[:, t, :], hbn[:, t, :]).then_inc(hstat, 1)

            def hnt_part(g, t):
                dve.wait_ge(hnt_hi, 4 * g + t + 1)
                STT(hntl[:, t, :], bank[HNT_BANK[t]][:, :], HS, hnth[:, t, :], ALU.mult, ALU.subtract).then_inc(hnt_lo, 1)

            def v_part(g, j):
                dve.wait_ge(v_hi, 2 * g + j + 1)
                s = slice(CG * j, CG * j + CG)
                STT(vl[:, s, :], bank[V_BANK[j]][:, :].rearrange("p (t d) -> p t d", t=CG), VS, vh[:, s, :],
                    ALU.mult, ALU.subtract).then_inc(v_lo, 1)

            def ct_part(f, j):
                dve.wait_ge(ct_hi, 2 * f + j + 1)
                s = slice(256 * j, 256 * j + 256)
                TT(ctl[:, :, s], bank[CT_BANK[j]][:, :].rearrange("p (k c) -> p k c", k=KD), cth[:, :, s],
                   ALU.subtract).then_inc(ct_lo, 1)

            def y_part(f, j):
                dve.wait_ge(o_rdy, 2 * f + j + 1)
                if j == 0:
                    dve.wait_ge(x2o_dn, f + 1)
                s = slice(CG * j, CG * j + CG)
                STT(y[:, s, :], bank[O_BANK[j]][:, :].rearrange("p (t d) -> p t d", t=CG), ksc[:, 3:4], x2o[:, s, :],
                    ALU.mult, ALU.add).then_inc(y_dn, 1)

            def body(dve, g, conv, ffn, prep):
                f = g - 1
                if conv:
                    dve.wait_ge(ht_cp, 4 * g + 4)
                    TS(dmax[:, :], deg[:, :], 1.0, None, ALU.max).then_inc(be_max, 1)
                    dve.wait_ge(be_max, g + 1)
                    v.reciprocal(be[:, :], dmax[:, :]).then_inc(be_dn, 1)
                    for e in range(CT):
                        if e % CG == 0:
                            dve.wait_ge(a1_hi, 4 * g + e + CG)
                        STT(a1l[:, e, :], bank[A1_BANK[e // CG]][:, 256 * (e % CG):256 * (e % CG) + 256],
                            be[:, e:e + 1], a1h[:, e, :], ALU.mult, ALU.subtract).then_inc(a1_lo, 1)
                    dve.wait_ge(d_rdy, g + 1)
                    v.reduce_sum(dsum[:, :], bank[D_BANK][:, 0:CT * 4].rearrange("p (t w) -> p t w", w=4)[:, :, 0:3],
                                 X).then_inc(d_step, 1)
                    dve.wait_ge(d_step, 6 * g + 1)
                    TS(dclip[:, :], dsum[:, :], 1.2e-38, None, ALU.max).then_inc(d_step, 1)
                    dve.wait_ge(d_step, 6 * g + 2)
                    v.reciprocal(drec[:, :], dclip[:, :]).then_inc(d_step, 1)
                    dve.wait_ge(d_step, 6 * g + 3)
                    STT(dn[:, :], dsum[:, :], 0.0, drec[:, :], ALU.is_gt, ALU.mult).then_inc(d_step, 1)
                    dve.wait_ge(d_step, 6 * g + 4)
                    TS(dna[:, :], dn[:, :], ksc[:, 0:1], None, ALU.mult).then_inc(d_step, 1)
                    TS(dnb[:, :], dn[:, :], ksc[:, 1:2], None, ALU.mult).then_inc(d_step, 1)
                if ffn:
                    for j in range(2):
                        dve.wait_ge(xt_hi, 2 * f + j + 1)
                        s = slice(256 * j, 256 * j + 256)
                        STT(xtl[:, :, s], bank[XT_BANK[j]][:, :].rearrange("p (k c) -> p k c", k=KD), XS,
                            xth[:, :, s], ALU.mult, ALU.subtract).then_inc(xt_lo, 1)
                if conv:
                    for k in range(KD):
                        dve.wait_ge(a2_hi, 2 * g + k + 1)
                        STT(a2l[:, k, :], bank[A2_BANK[k]][:, :], A2S, a2h[:, k, :], ALU.mult,
                            ALU.subtract).then_inc(a2_lo, 1)
                if prep:
                    prep_x_stats(g + 1)
                if ffn:
                    dve.wait_ge(lg_rdy, f + 1)
                    STT(lg[:, :, :], bank[R_BANK][:, 0:CT * NE].rearrange("p (t e) -> p t e", e=NE), ksc[:, 4:5],
                        rbb[:, :, :], ALU.mult, ALU.add).then_inc(lg_dn, 1)
                    dve.wait_ge(lg_dn, f + 1)
                    TT(ldf[:, :, :, :], lg[:, :, :].unsqueeze(2).to_broadcast([P, CT, NE, NE]),
                       lg[:, :, :].unsqueeze(3).to_broadcast([P, CT, NE, NE]), ALU.subtract).then_inc(r_step, 1)
                if prep:
                    prep_x_aggr(g + 1)
                if ffn:
                    flat = (lambda t: t[:, :, :, :].rearrange("p t e j -> p (t e j)"))
                    dve.wait_ge(r_step, 8 * f + 1)
                    STT(flat(tie), flat(ldf), 0.0, flat(tri), ALU.is_ge, ALU.mult).then_inc(r_step, 1)
                    dve.wait_ge(r_step, 8 * f + 2)
                    STT(flat(beat), flat(ldf), 0.0, flat(tie), ALU.is_gt, ALU.max).then_inc(r_step, 1)
                    dve.wait_ge(r_step, 8 * f + 3)
                    v.reduce_sum(rank[:, :, :], beat[:, :, :, :], X).then_inc(r_step, 1)
                    dve.wait_ge(r_step, 8 * f + 4)
                    STT(lsel[:, :, :], rank[:, :, :], 1.5, lg[:, :, :], ALU.is_lt, ALU.mult).then_inc(r_step, 1)
                    dve.wait_ge(r_step, 8 * f + 5)
                    v.reduce_sum(lsum[:, :], lsel[:, :, :], X).then_inc(r_step, 1)
                    dve.wait_ge(r_step, 8 * f + 6)
                    STT(arg[:, :, :], lsum[:, :].unsqueeze(2).to_broadcast([P, CT, NE]), -0.5, lg[:, :, :],
                        ALU.mult, ALU.add).then_inc(arg_dn, 1)
                    dve.wait_ge(th_dn, f + 1)
                    TS(wt[:, :, :], th[:, :, :], ksc[:, 5:6], ksc[:, 6:7], ALU.mult, ALU.add).then_inc(r_step, 1)
                    dve.wait_ge(r_step, 8 * f + 7)
                    STT(mask[:, :, :], rank[:, :, :], 1.5, wt[:, :, :], ALU.is_lt, ALU.mult).then_inc(r_step, 1)
                    dve.wait_ge(r_step, 8 * f + 8)
                    combine(f, 0)
                if prep:
                    prep_x_lo(g + 1)
                if conv:
                    dve.wait_ge(d_step, 6 * g + 6)
                    z_part(g, 0)
                    z_part(g, 1)
                    h_stats(g, 0)
                    z_part(g, 2)
                    h_stats(g, 1)
                    dve.wait_ge(hbn_dn, 4 * g + 1)
                    z_part(g, 3)
                    h_aggr(g, 0)
                    dve.wait_ge(hbn_dn, 4 * g + 2)
                    h_stats(g, 2)
                    h_aggr(g, 1)
                    dve.wait_ge(hbn_dn, 4 * g + 3)
                    h_stats(g, 3)
                    h_aggr(g, 2)
                    dve.wait_ge(hbn_dn, 4 * g + 4)
                    v.memset(spare[:, :], 0.0)
                if ffn:
                    combine(f, 1)
                if conv:
                    h_aggr(g, 3)
                if ffn:
                    combine(f, 2)
                    combine(f, 3)
                if conv:
                    hnt_part(g, 0)
                    hnt_part(g, 1)
                    hnt_part(g, 2)
                    v_part(g, 0)
                    hnt_part(g, 3)
                if ffn:
                    ct_part(f, 0)
                if conv:
                    v_part(g, 1)
                if ffn:
                    ct_part(f, 1)
                    y_part(f, 0)
                if conv:
                    for e in range(CT):
                        if e % CG == 0:
                            dve.wait_ge(u_hi, 4 * g + e + CG)
                        STT(ul[:, e, :], bank[U_BANK[e // CG]][:, 256 * (e % CG):256 * (e % CG) + 256],
                            be[:, e:e + 1], uh[:, e, :], ALU.mult, ALU.subtract).then_inc(u_lo, 1)
                if ffn:
                    y_part(f, 1)
                if prep:
                    prep_h(g + 1)
                if conv:
                    dve.wait_ge(xb_st, 2 * g + 2)
                    if ffn:
                        dve.wait_ge(x1_kept, f + 1)
                    for j in range(2):
                        dve.wait_ge(b3_rdy, 2 * g + j + 1)
                        for t in range(CG * j, CG * j + CG):
                            STT(x1[:, t, :], bank[B3_BANK[j]][:, 256 * (t % CG):256 * (t % CG) + 256],
                                dnb[:, t:t + 1], xb[:, t, :], ALU.mult, ALU.add).then_inc(x1_dn, 1)
                        for t in range(CG * j, CG * j + CG):
                            dve.wait_ge(x1_dn, 4 * g + t + 1)
                            v.bn_stats(ybn[:, t, :], x1[:, t, :]).then_inc(ybn_dn, 1)
                if ffn:
                    dve.wait_ge(rr_st, 3 * f + 3)
                    for t in range(CT):
                        if t == 1 and conv:
                            dve.wait_ge(ybn_dn, 4 * g + 4)
                        STT(yf[:, t, :], y[:, t, :], yrr[:, t:t + 1], nwb[:, :], ALU.mult, ALU.mult).then_inc(yf_dn, 1)
                        if t == 1 and conv:
                            for a in range(CT):
                                ins = v.bn_aggr(ymv[:, a, :], ybn[:, a, :])
                            ins.then_inc(ystat, 1)
                elif conv:
                    dve.wait_ge(ybn_dn, 4 * g + 4)
                    v.memset(spare[:, :], 0.0)
                    for a in range(CT):
                        ins = v.bn_aggr(ymv[:, a, :], ybn[:, a, :])
                    ins.then_inc(ystat, 1)
            steps(dve, body, None)

        @block.tensor
        def _(pe):
            mm = nc.tensor.matmul

            def three(outp, lh, ll, rh, rl, first, last):
                mm(outp, lh, rh, start=first, stop=False)
                mm(outp, lh, rl, start=False, stop=False)
                return mm(outp, ll, rh, start=False, stop=last)

            pe.wait_ge(w_in, 16 * NWEIGHTS)
            for k in range(KH):
                ins = mm(bank[0][0:1, 0:D], bet[:, k:k + 1], w2f[:, k, :], start=(k == 0), stop=(k == KH - 1))
            ins.then_inc(c_pe, 1)

            def experts(f, t):
                for p in range(2):
                    i = 2 * t + p
                    b = bank[E_BANK[i]][:, :]
                    if i == 2:
                        pe.wait_ge(lg_dn, f + 1)
                    if i >= 3:
                        pe.wait_ge(silu_dn, 8 * f + i - 2)
                    mm(b, ones[:, :], ebias[:, 512 * p:512 * p + 512], start=True, stop=False)
                    for k in range(KD):
                        ins = three(b, xth[:, k, P * t:P * t + P], xtl[:, k, P * t:P * t + P],
                                    ewh[:, k, 512 * p:512 * p + 512], ewl[:, k, 512 * p:512 * p + 512], False, k == KD - 1)
                    ins.then_inc(e_rdy, 1)

            def transposed_h(g, t):
                pe.wait_ge(hn_dn, 4 * g + t + 1)
                if t >= 2:
                    pe.wait_ge(hnt_lo, 4 * g + t - 1)
                for k in range(KH):
                    ins = nc.tensor.transpose(bank[HNT_BANK[t]][:, P * k:P * k + P], hn[:, t, P * k:P * k + P], ident[:, :])
                ins.then_inc(hnt_rdy, 1)

            def v_tile(g, t):
                pe.wait_ge(hnt_lo, 4 * g + t + 1)
                if t == 0:
                    pe.wait_ge(z_dn, 4 * g + 4)
                b = bank[V_BANK[t // CG]][:, D * (t % CG):D * (t % CG) + D]
                mm(b, ones[:, :], vbias[:, :], start=True, stop=False)
                for k in range(KH):
                    ins = three(b, hnth[:, t, P * k:P * k + P], hntl[:, t, P * k:P * k + P], w2h[:, k, :], w2l[:, k, :],
                                False, k == KH - 1)
                if t % CG == CG - 1:
                    ins.then_inc(v_rdy, 1)

            def transposed_comb(f, j):
                if j == 0:
                    pe.wait_ge(silu_dn, 8 * f + 6)
                pe.wait_ge(comb_st, 16 * f + 4 * (CG * j + CG))
                for k in range(KD):
                    for t in range(CG):
                        ins = nc.tensor.transpose(bank[CT_BANK[j]][:, 256 * k + P * t:256 * k + P * t + P],
                                                  comb[:, CG * j + t, P * k:P * k + P], ident[:, :])
                ins.then_inc(ct_rdy, 1)

            def out_product(f, j):
                pe.wait_ge(ct_lo, 2 * f + j + 1)
                for t in range(CG * j, CG * j + CG):
                    b = bank[O_BANK[j]][:, D * (t % CG):D * (t % CG) + D]
                    for k in range(KD):
                        ins = three(b, cth[:, k, P * t:P * t + P], ctl[:, k, P * t:P * t + P], owh[:, k, :], owl[:, k, :],
                                    k == 0, k == KD - 1)
                ins.then_inc(o_rdy, 1)

            def incidence(g, banks, weights, hi, lo, s_rdy):
                for e in range(CT):
                    b = bank[banks[e // CG]][:, D * (e % CG):D * (e % CG) + D]
                    for k in range(CT):
                        mm(b, weights[:, k, P * e:P * e + P], hi[:, k, :], start=(k == 0), stop=False)
                        ins = mm(b, weights[:, k, P * e:P * e + P], lo[:, k, :], start=False, stop=(k == CT - 1))
                    if e % CG == CG - 1:
                        ins.then_inc(s_rdy, 1)

            def body(pe, g, conv, ffn, prep):
                f = g - 1
                if conv:
                    pe.wait_ge(h_made, g + 1)
                    for k in range(CT):
                        if ffn:
                            if k == 0:
                                pe.wait_ge(hnt_lo, 4 * g)
                            elif k == 1:
                                pe.wait_ge(v_lo, 2 * g)
                            elif k == 2:
                                pe.wait_ge(u_lo, 4 * (g - 1) + 2)
                            else:
                                pe.wait_ge(x1_dn, 4 * (g - 1) + 2)
                        for c in range(CT):
                            ins = nc.tensor.transpose(bank[HT_BANK[k]][:, 0:256].bitcast(F16)[:, P * c:P * c + P],
                                                      h16[:, c, P * k:P * k + P], ident16[:, :])
                        ins.then_inc(ht_rdy, 1)
                    pe.wait_ge(xs_lo, g + 1)
                    pe.wait_ge(ht_cp, 4 * g + 2)
                    incidence(g, A1_BANK, h16, xsh, xsl, a1_rdy)
                    pe.wait_ge(ht_cp, 4 * g + 4)
                    pe.wait_ge(w_cur, g + 1)
                    if ffn:
                        pe.wait_ge(x1_dn, 4 * g)
                    for t in range(CT):
                        for k in range(CT):
                            ins = mm(bank[D_BANK][:, 4 * t:4 * t + 3], ht16[:, k, P * t:P * t + P], wcur[:, k, :],
                                     start=(k == 0), stop=(k == CT - 1))
                    ins.then_inc(d_rdy, 1)
                if ffn:
                    for j in range(2):
                        pe.wait_ge(x2_dn, 4 * f + CG * j + CG)
                        for k in range(KD):
                            for t in range(CG):
                                ins = nc.tensor.transpose(bank[XT_BANK[j]][:, 256 * k + P * t:256 * k + P * t + P],
                                                          x2[:, CG * j + t, P * k:P * k + P], ident[:, :])
                        ins.then_inc(xt_rdy, 1)
                if conv:
                    pe.wait_ge(a1_lo, 4 * g + 4)
                    for d in range(KD):
                        for k in range(CT):
                            mm(bank[A2_BANK[d]][:, :], a1h[:, k, P * d:P * d + P], ht16[:, k, :], start=(k == 0), stop=False)
                            ins = mm(bank[A2_BANK[d]][:, :], a1l[:, k, P * d:P * d + P], ht16[:, k, :], start=False,
                                     stop=(k == CT - 1))
                        ins.then_inc(a2_rdy, 1)
                if ffn:
                    pe.wait_ge(xt_lo, 2 * f + 2)
                    for t in range(CT):
                        for k in range(KD):
                            ins = three(bank[R_BANK][:, NE * t:NE * t + NE], xth[:, k, P * t:P * t + P],
                                        xtl[:, k, P * t:P * t + P], rwh[:, k, :], rwl[:, k, :], k == 0, k == KD - 1)
                    ins.then_inc(lg_rdy, 1)
                    experts(f, 0)
                if conv:
                    pe.wait_ge(a2_lo, 2 * g + 2)
                    for t in range(CT):
                        for k in range(KD):
                            ins = three(bank[A3_BANK[t]][:, :], a2h[:, k, P * t:P * t + P], a2l[:, k, P * t:P * t + P],
                                        w1h[:, k, :], w1l[:, k, :], k == 0, k == KD - 1)
                        ins.then_inc(a3_rdy, 1)
                if ffn:
                    for t in range(1, CT):
                        experts(f, t)
                if conv:
                    transposed_h(g, 0)
                    transposed_h(g, 1)
                    v_tile(g, 0)
                    transposed_h(g, 2)
                    v_tile(g, 1)
                    transposed_h(g, 3)
                    v_tile(g, 2)
                if ffn:
                    transposed_comb(f, 0)
                if conv:
                    v_tile(g, 3)
                if ffn:
                    transposed_comb(f, 1)
                    out_product(f, 0)
                if conv:
                    pe.wait_ge(v_lo, 2 * g + 2)
                    incidence(g, U_BANK, h16, vh, vl, u_rdy)
                if ffn:
                    out_product(f, 1)
                if conv:
                    pe.wait_ge(u_lo, 4 * g + 4)
                    incidence(g, B3_BANK, ht16, uh, ul, b3_rdy)

            pe.wait_ge(c_pool, 11)
            pe.wait_ge(c_dve, 4)
            steps(pe, body, None)


def kernel(x, adj, L0_gnn_W1, L0_gnn_b1, L0_gnn_gamma, L0_gnn_beta, L0_gnn_W2, L0_gnn_b2, L0_ffn_router_w,
           L0_ffn_router_b, L0_ffn_expert_w, L0_ffn_expert_b, L0_ffn_out_w, L0_ffn_out_b, L0_ffn_norm_w):
    import numpy as np
    import concourse.bacc as bacc
    from concourse.bass_utils import run_bass_kernel_spmd

    def arr(a):
        return np.ascontiguousarray(a)

    x, adj = np.asarray(x), np.asarray(adj)
    n, c, d = x.shape
    dh = L0_gnn_b1.shape[0]
    ne = L0_ffn_expert_w.shape[0]
    arrays = {
        "x": arr(x),
        "adj": arr(adj),
        "wrow": arr(adj[:, 0, :].reshape(n, c // P, P).transpose(2, 0, 1)),
        "w1t": arr(np.asarray(L0_gnn_W1).T),
        "b1": arr(np.asarray(L0_gnn_b1).reshape(1, dh)),
        "gamma": arr(np.asarray(L0_gnn_gamma).reshape(dh // P, P).T),
        "beta": arr(np.asarray(L0_gnn_beta).reshape(dh // P, P).T),
        "w2t": arr(np.asarray(L0_gnn_W2).T),
        "b2": arr(np.asarray(L0_gnn_b2).reshape(1, d)),
        "rw": arr(L0_ffn_router_w),
        "rb": arr(np.asarray(L0_ffn_router_b).reshape(1, ne)),
        "ew": arr(np.asarray(L0_ffn_expert_w).transpose(1, 0, 2)),
        "eb": arr(np.asarray(L0_ffn_expert_b).reshape(1, ne * d)),
        "ow": arr(L0_ffn_out_w),
        "ob": arr(np.asarray(L0_ffn_out_b).reshape(1, d)),
        "nw": arr(np.asarray(L0_ffn_norm_w).reshape(1, d)),
    }
    nc = bacc.Bacc("TRN2", target_bir_lowering=False, num_devices=1)
    args = [nc.dram_tensor(k, a.shape, mybir.dt.from_np(a.dtype), kind="ExternalInput").ap() for k, a in arrays.items()]
    res = nc.dram_tensor("out", (n, c, d), F32, kind="ExternalOutput").ap()
    build(nc, *args, res)
    got = run_bass_kernel_spmd(nc, [arrays], core_ids=[0])
    return got.results[0]["out"]
```

```python
from contextlib import ExitStack

import concourse.bass as bass
from concourse import mybir

ALU = mybir.AluOpType
ACT = mybir.ActivationFunctionType
F32 = mybir.dt.float32
F16 = mybir.dt.float16
BF16 = mybir.dt.bfloat16
I32 = mybir.dt.int32
X = mybir.AxisListType.X
RMAX = bass.bass_isa.ReduceOp.max

P = 128
EPS_LN = 1e-5
EPS_RMS = 1e-6

XS = 2.0 ** 11
A2S = 2.0 ** -9
HS = 2.0 ** 10
WS = 2.0 ** 13
VS = 2.0 ** -19


def build(nc, x, adj, wrow, w1t, b1, gamma, beta, w2t, b2, rw, rb, ew, eb, ow, ob, nw, out):
    N, C, D = x.shape
    DH = w1t.shape[1]
    NE = ew.shape[1]
    CT, KD, KH = C // P, D // P, DH // P
    CG = 2
    assert (C, D, DH, NE) == (512, 256, 512, 4)

    with ExitStack() as ctx:
        def sb(name, shape, dt):
            return ctx.enter_context(nc.sbuf_tensor(name, shape, dt))

        def sem(name):
            return ctx.enter_context(nc.semaphore(name))

        bank = [ctx.enter_context(nc.psum_tensor(f"bank{i}", [P, 512], F32)) for i in range(8)]
        HT_BANK, A1_BANK, D_BANK, A2_BANK = (0, 3, 4, 1), (0, 3), 2, (4, 1)
        A3_BANK, HNT_BANK, V_BANK, U_BANK, B3_BANK = (0, 3, 4, 1), (2, 0, 2, 0), (1, 2), (3, 4), (1, 2)
        XT_BANK, R_BANK, E_BANK, CT_BANK, O_BANK = (5, 6), 7, (5, 6, 7, 5, 6, 7, 5, 6), (7, 5), (6, 7)

        w1f = sb("w1f", [P, KD, DH], F32)
        w2f = sb("w2f", [P, KH, D], F32)
        w2g = sb("w2g", [P, KH, D], F32)
        ewf = sb("ewf", [P, KD, NE * D], F32)
        owf = sb("owf", [P, KD, D], F32)
        rwf = sb("rwf", [P, KD, NE], F32)
        w1h, w1l = sb("w1h", [P, KD, DH], F16), sb("w1l", [P, KD, DH], F16)
        w2h, w2l = sb("w2h", [P, KH, D], F16), sb("w2l", [P, KH, D], F16)
        ewh, ewl = sb("ewh", [P, KD, NE * D], F16), sb("ewl", [P, KD, NE * D], F16)
        owh, owl = sb("owh", [P, KD, D], F16), sb("owl", [P, KD, D], F16)
        rwh, rwl = sb("rwh", [P, KD, NE], F16), sb("rwl", [P, KD, NE], F16)
        gam, bet = sb("gam", [P, KH], F32), sb("bet", [P, KH], F32)
        b1b = sb("b1b", [P, DH], F32)
        b2b, obb = sb("b2b", [P, D], F32), sb("obb", [P, D], F32)
        nwb = sb("nwb", [P, D], F32)
        rbb = sb("rbb", [P, CT, NE], F32)
        ebrow = sb("ebrow", [1, NE * D], F32)
        brow = sb("brow", [1, NE * D], F32)
        bwrow = sb("bwrow", [1, D], F32)
        ebias = sb("ebias", [P, NE * D], BF16)
        vbias = sb("vbias", [P, D], BF16)
        ones = sb("ones", [P, P], BF16)
        absbuf = sb("absbuf", [P, 2048], F32)
        mags = sb("mags", [P, 8], F32)
        pmax = sb("pmax", [P, 8], F32)
        pw = sb("pw", [P, 8], F32)
        ipw = sb("ipw", [P, 8], F32)
        wsc = sb("wsc", [P, 8], F32)
        ksc = sb("ksc", [P, 8], F32)
        ident = sb("ident", [P, P], F32)
        ident16 = sb("ident16", [P, P], F16)
        epsln, epsrms = sb("epsln", [P, CT], F32), sb("epsrms", [P, CT], F32)
        mhalf, mone = sb("mhalf", [P, CT], F32), sb("mone", [P, CT], F32)
        tri = sb("tri", [P, CT, NE, NE], F32)
        wf = sb("wf", [P, N, CT], F32)
        wr1, wr2 = sb("wr1", [P, N, CT], F32), sb("wr2", [P, N, CT], F32)
        wparts = sb("wparts", [P, N, CT, 3], BF16)

        xin = sb("xin", [P, CT, D], F32)
        adjin = sb("adjin", [P, CT, C], F32)
        h16 = sb("h16", [P, CT, C], F16)
        ht16 = sb("ht16", [P, CT, C], F16)
        wcur = sb("wcur", [P, CT, 3], BF16)
        xbn = sb("xbn", [P, CT, 6], F32)
        xmv = sb("xmv", [P, CT, 2], F32)
        xve, xrs, xnm, xnb = (sb(n, [P, CT], F32) for n in ("xve", "xrs", "xnm", "xnb"))
        xn = sb("xn", [P, CT, D], F32)
        xsh, xsl = sb("xsh", [P, CT, D], F16), sb("xsl", [P, CT, D], F16)
        xsum = sb("xsum", [P, CT, D], F32)
        xb = sb("xb", [P, CT, D], F32)
        deg, dmax, be = (sb(n, [P, CT], F32) for n in ("deg", "dmax", "be"))
        dsum, dclip, drec, dn, dna, dnb = (sb(n, [P, CT], F32) for n in ("dsum", "dclip", "drec", "dn", "dna", "dnb"))
        a1h, a1l = sb("a1h", [P, CT, D], F16), sb("a1l", [P, CT, D], F16)
        a2h, a2l = sb("a2h", [P, KD, C], F16), sb("a2l", [P, KD, C], F16)
        z = sb("z", [P, CT, DH], F32)
        r = sb("r", [P, CT, DH], F32)
        hbn = sb("hbn", [P, CT, 6], F32)
        hmv = sb("hmv", [P, CT, 2], F32)
        hve, hrs, hnm, hnb = (sb(n, [P, CT], F32) for n in ("hve", "hrs", "hnm", "hnb"))
        hn = sb("hn", [P, CT, DH], F32)
        hnth, hntl = sb("hnth", [P, CT, KH * P], F16), sb("hntl", [P, CT, KH * P], F16)
        vh, vl = sb("vh", [P, CT, D], F16), sb("vl", [P, CT, D], F16)
        uh, ul = sb("uh", [P, CT, D], F16), sb("ul", [P, CT, D], F16)
        x1 = sb("x1", [P, CT, D], F32)
        ybn = sb("ybn", [P, CT, 6], F32)
        ymv = sb("ymv", [P, CT, 2], F32)
        yve, yrs, ynm, ynb = (sb(n, [P, CT], F32) for n in ("yve", "yrs", "ynm", "ynb"))

        x1k = sb("x1k", [P, CT, D], F32)
        x2 = sb("x2", [P, CT, D], F32)
        x2o = sb("x2o", [P, CT, D], F32)
        xth, xtl = sb("xth", [P, KD, C], F16), sb("xtl", [P, KD, C], F16)
        spare = sb("spare", [P, 1], F32)
        lg = sb("lg", [P, CT, NE], F32)
        ldf, tie, beat = (sb(n, [P, CT, NE, NE], F32) for n in ("ldf", "tie", "beat"))
        rank, lsel, arg, th, wt, mask = (sb(n, [P, CT, NE], F32) for n in ("rank", "lsel", "arg", "th", "wt", "mask"))
        lsum = sb("lsum", [P, CT], F32)
        silu = sb("silu", [P, 4, 512], F32)
        comb = sb("comb", [P, CT, D], F32)
        cth, ctl = sb("cth", [P, KD, C], F16), sb("ctl", [P, KD, C], F16)
        y = sb("y", [P, CT, D], F32)
        ysq = sb("ysq", [P, D], F32)
        yms, yme, yrr = (sb(n, [P, CT], F32) for n in ("yms", "yme", "yrr"))
        yf = sb("yf", [P, CT, D], F32)
        outb = sb("outb", [P, CT, D], F32)

        w_in, c_pool, c_dve, c_act, c_pe = (sem(n) for n in ("w_in", "c_pool", "c_dve", "c_act", "c_pe"))

        x_in, adj_in, out_st = sem("x_in"), sem("adj_in"), sem("out_st")
        ht_rdy, a3_rdy, hnt_rdy = sem("ht_rdy"), sem("a3_rdy"), sem("hnt_rdy")
        a1_rdy, a2_rdy, v_rdy, u_rdy, b3_rdy = (sem(n) for n in ("a1_rdy", "a2_rdy", "v_rdy", "u_rdy", "b3_rdy"))
        xt_rdy, ct_rdy, o_rdy = sem("xt_rdy"), sem("ct_rdy"), sem("o_rdy")
        d_rdy, lg_rdy = sem("d_rdy"), sem("lg_rdy")
        e_rdy = sem("e_rdy")
        ht_cp, a1_hi, relu_dn, hn_dn, hnt_hi, u_hi, x2_dn, sq_dn, xn_dn = (
            sem(n) for n in ("ht_cp", "a1_hi", "relu_dn", "hn_dn", "hnt_hi", "u_hi", "x2_dn", "sq_dn", "xn_dn"))
        a2_hi, v_hi, xt_hi, ct_hi = (sem(n) for n in ("a2_hi", "v_hi", "xt_hi", "ct_hi"))
        xs_hi, th_dn = sem("xs_hi"), sem("th_dn")
        silu_dn = sem("silu_dn")
        h_made, be_max, be_dn, xs_lo, xstat, lg_dn, arg_dn, mask_dn = (
            sem(n) for n in ("h_made", "be_max", "be_dn", "xs_lo", "xstat", "lg_dn", "arg_dn", "mask_dn"))
        d_step = sem("d_step")
        r_step = sem("r_step")
        a1_lo, z_dn, hbn_dn, hstat, hnt_lo, u_lo, x1_dn, ybn_dn, xbn_dn, yf_dn = (
            sem(n) for n in ("a1_lo", "z_dn", "hbn_dn", "hstat", "hnt_lo", "u_lo", "x1_dn", "ybn_dn", "xbn_dn", "yf_dn"))
        ystat = sem("ystat")
        a2_lo, v_lo, xt_lo, ct_lo, y_dn = (sem(n) for n in ("a2_lo", "v_lo", "xt_lo", "ct_lo", "y_dn"))
        comb_st = sem("comb_st")
        xrs_st, yrs_st = sem("xrs_st"), sem("yrs_st")
        hrs_st = sem("hrs_st")
        rr_st = sem("rr_st")
        xs_sum, xb_dn = sem("xs_sum"), sem("xb_dn")
        w_cur, x1_kept, x2o_dn = sem("w_cur"), sem("x1_kept"), sem("x2o_dn")
        out_rdy = sem("out_rdy")

        def steps(eng, body):
            body(eng, 0, conv=True, ffn=False, late=False, prep=True)
            body(eng, 1, conv=True, ffn=True, late=False, prep=True)
            with eng.Fori(2, N - 1) as g:
                body(eng, g, conv=True, ffn=True, late=True, prep=True)
            body(eng, N - 1, conv=True, ffn=True, late=True, prep=False)
            body(eng, N, conv=False, ffn=True, late=True, prep=False)
            body(eng, N + 1, conv=False, ffn=False, late=True, prep=False)

        block = ctx.enter_context(nc.Block())

        NWEIGHTS = 14


        @block.sync
        def _(sp):
            sp.dma_start(xin[:, :, :], x[0].rearrange("(t p) d -> p t d", p=P)).then_inc(x_in, 16)
            sp.dma_start(adjin[:, :, :], adj[0].rearrange("(t p) e -> p t e", p=P)).then_inc(adj_in, 16)
            for dst, src in (
                (w2f[:, :, :], w2t.rearrange("(k p) f -> p k f", p=P)),
                (gam[:, :], gamma), (bet[:, :], beta),
                (w1f[:, :, :], w1t.rearrange("(k p) h -> p k h", p=P)),
                (ewf[:, :, :].rearrange("p k (e h) -> p k e h", e=NE), ew.rearrange("(k p) e h -> p k e h", p=P)),
                (owf[:, :, :], ow.rearrange("(k p) h -> p k h", p=P)),
                (rwf[:, :, :], rw.rearrange("(k p) e -> p k e", p=P)),
                (ebrow[:, :], eb), (wf[:, :, :], wrow),
                (b1b[:, :], b1.to_broadcast([P, DH])),
                (b2b[:, :], b2.to_broadcast([P, D])), (obb[:, :], ob.to_broadcast([P, D])),
                (nwb[:, :], nw.to_broadcast([P, D])), (rbb[:, 0, :], rb.to_broadcast([P, NE])),
            ):
                sp.dma_start(dst, src).then_inc(w_in, 16)

            def body(sp, g, conv, ffn, late, prep):
                if prep:
                    sp.wait_ge(xs_sum, g + 1)
                    sp.dma_start(xin[:, :, :], x[g + 1].rearrange("(t p) d -> p t d", p=P)).then_inc(x_in, 16)
                    sp.wait_ge(h_made, g + 1)
                    sp.dma_start(adjin[:, :, :], adj[g + 1].rearrange("(t p) e -> p t e", p=P)).then_inc(adj_in, 16)
                if late:
                    q = g - 2
                    for j in range(2):
                        sp.wait_ge(out_rdy, 2 * q + j + 1)
                        sp.dma_start(out[q].rearrange("(t p) d -> p t d", p=P)[:, CG * j:CG * j + CG, :],
                                     outb[:, CG * j:CG * j + CG, :]).then_inc(out_st, 16)
            steps(sp, body)
            sp.wait_ge(out_st, 32 * N)

        @block.gpsimd
        def _(gp):
            tt = nc.gpsimd.tensor_tensor
            nc.gpsimd.memset(ident[:, :], 0.0).then_inc(c_pool, 1)
            nc.gpsimd.memset(ident16[:, :], 0.0).then_inc(c_pool, 1)
            nc.gpsimd.memset(tri[:, :, :, :], 1.0).then_inc(c_pool, 1)
            for t, v in ((epsln, EPS_LN), (epsrms, EPS_RMS), (mhalf, -0.5), (mone, -1.0)):
                nc.gpsimd.memset(t[:, :], v).then_inc(c_pool, 1)
            gp.wait_ge(c_pool, 7)
            for m in (ident, ident16):
                gp.affine_select(out=m[:, :], in_=m[:, :], compare_op=ALU.not_equal, fill=1.0, base=0,
                                 pattern=[[-1, P]], channel_multiplier=1).then_inc(c_pool, 1)
            gp.affine_select(out=tri[:, :, :, :], in_=tri[:, :, :, :], compare_op=ALU.is_gt, fill=0.0, base=0,
                             pattern=[[0, CT], [1, NE], [-1, NE]], channel_multiplier=0).then_inc(c_pool, 1)

            def root(stat, mv, ve, rs, nm, nb, sem_st, g, per, k, s, stat_per, stat_k):
                gp.wait_ge(stat, stat_per * g + stat_k)
                tt(ve[:, s], mv[:, s, 1], epsln[:, s], ALU.add).then_inc(sem_st, 1)
                tt(nm[:, s], mv[:, s, 0], mone[:, s], ALU.mult).then_inc(sem_st, 1)
                gp.wait_ge(sem_st, per * g + k + 2)
                tt(rs[:, s], ve[:, s], mhalf[:, s], ALU.pow).then_inc(sem_st, 1)
                gp.wait_ge(sem_st, per * g + k + 3)
                tt(nb[:, s], nm[:, s], rs[:, s], ALU.mult).then_inc(sem_st, 1)

            ALL = slice(0, CT)

            def prep_x(g, again=True):
                if again:
                    gp.wait_ge(d_rdy, g)
                root(xstat, xmv, xve, xrs, xnm, xnb, xrs_st, g, 4, 0, ALL, 1, 1)
                nc.gpsimd.tensor_copy(wcur[:, :, :], wparts[:, g, :, :]).then_inc(w_cur, 1)

            def sum_x(g, again=True):
                gp.wait_ge(xn_dn, 4 * g + 4)
                if again:
                    gp.wait_ge(xb_dn, g)
                tt(xsum[:, :, :], xin[:, :, :], xn[:, :, :], ALU.add).then_inc(xs_sum, 1)

            def make_xb(g, again=True):
                if again:
                    gp.wait_ge(x1_dn, 4 * g)
                gp.wait_ge(xs_sum, g + 1)
                tt(xb[:, :, :], xsum[:, :, :], b2b[:, :].unsqueeze(1).to_broadcast([P, CT, D]), ALU.add).then_inc(xb_dn, 1)

            gp.wait_ge(c_dve, 1)
            nc.gpsimd.partition_all_reduce(pmax[:, :], mags[:, :], P, RMAX).then_inc(c_pool, 1)
            gp.wait_ge(w_in, 16 * NWEIGHTS)
            gp.wait_ge(c_dve, 2)
            prep_x(0, again=False)
            sum_x(0, again=False)
            make_xb(0, again=False)

            def body(gp, g, conv, ffn, late, prep):
                f, q = g - 1, g - 2
                if late:
                    for j in range(2):
                        s = slice(CG * j, CG * j + CG)
                        gp.wait_ge(yf_dn, 4 * q + CG * j + CG)
                        tt(outb[:, s, :], yf[:, s, :], x1k[:, s, :], ALU.add).then_inc(out_rdy, 1)
                if prep:
                    prep_x(g + 1)
                if ffn:
                    gp.wait_ge(x2_dn, 4 * f + 4)
                    tt(x2o[:, :, :], x2[:, :, :], obb[:, :].unsqueeze(1).to_broadcast([P, CT, D]), ALU.add).then_inc(x2o_dn, 1)
                if prep:
                    sum_x(g + 1)
                if conv:
                    for t in range(CT):
                        root(hstat, hmv, hve, hrs, hnm, hnb, hrs_st, g, 16, 4 * t, slice(t, t + 1), 4, t + 1)
                if ffn:
                    if late:
                        gp.wait_ge(out_st, 32 * q + 32)
                    gp.wait_ge(sq_dn, 4 * f + 4)
                    tt(yme[:, :], yms[:, :], epsrms[:, :], ALU.add).then_inc(rr_st, 1)
                    gp.wait_ge(rr_st, 2 * f + 1)
                    tt(yrr[:, :], yme[:, :], mhalf[:, :], ALU.pow).then_inc(rr_st, 1)
                if conv:
                    for j in range(2):
                        root(ystat, ymv, yve, yrs, ynm, ynb, yrs_st, g, 8, 4 * j, slice(CG * j, CG * j + CG), 2, j + 1)
                if prep:
                    make_xb(g + 1)
            steps(gp, body)

        @block.scalar
        def _(act):
            af = nc.scalar.activation

            def prep_x(g, tiles, again=True):
                if tiles[0] == 0:
                    act.wait_ge(xrs_st, 4 * g + 4)
                    if again:
                        act.wait_ge(xs_sum, g)
                        act.wait_ge(xs_lo, g)
                for t in tiles:
                    af(xn[:, t, :], xin[:, t, :], ACT.Identity, bias=xnb[:, t:t + 1],
                       scale=xrs[:, t:t + 1]).then_inc(xn_dn, 1)

            def prep_x_hi(g, again=True):
                act.wait_ge(xn_dn, 4 * g + 4)
                if again:
                    act.wait_ge(a1_rdy, 2 * g)
                af(xsh[:, :, :], xn[:, :, :], ACT.Copy, scale=XS).then_inc(xs_hi, 1)

            act.wait_ge(c_pool, 7)
            af(ysq[:, 0:1], epsln[:, 0:1], ACT.Silu).then_inc(c_act, 1)
            prep_x(0, range(CT), again=False)
            prep_x_hi(0, again=False)
            act.wait_ge(c_dve, 3)
            for i, (full, hi) in enumerate(((w1f, w1h), (w2g, w2h), (ewf, ewh), (owf, owh), (rwf, rwh))):
                af(hi[:, :, :], full[:, :, :], ACT.Copy, scale=wsc[:, i:i + 1]).then_inc(c_act, 1)

            def hi_rows(dst, src, t, scale, s_hi):
                af(dst, src, ACT.Copy, scale=scale).then_inc(s_hi, 1)

            def expert(act, f, i):
                act.wait_ge(e_rdy, 8 * f + i + 1)
                if i >= 4:
                    act.wait_ge(comb_st, 16 * f + 4 * ((i - 4) // 2) + 4)
                af(silu[:, i % 4, :], bank[E_BANK[i]][:, :], ACT.Silu, scale=ksc[:, 2:3]).then_inc(silu_dn, 1)

            def relu(act, g, t):
                act.wait_ge(z_dn, 4 * g + t + 1)
                af(r[:, t, :], z[:, t, :], ACT.Relu).then_inc(relu_dn, 1)

            def norm_h(act, g, t):
                act.wait_ge(hrs_st, 16 * g + 4 * t + 4)
                af(hn[:, t, :], r[:, t, :], ACT.Identity, bias=hnb[:, t:t + 1],
                   scale=hrs[:, t:t + 1]).then_inc(hn_dn, 1)

            def hnt_part(act, g, t):
                act.wait_ge(hnt_rdy, 4 * g + t + 1)
                af(hnth[:, t, :], bank[HNT_BANK[t]][:, :], ACT.Copy, scale=HS).then_inc(hnt_hi, 1)

            def v_part(act, g, j):
                act.wait_ge(v_rdy, 2 * g + j + 1)
                af(vh[:, CG * j:CG * j + CG, :], bank[V_BANK[j]][:, :].rearrange("p (t d) -> p t d", t=CG),
                   ACT.Copy, scale=VS).then_inc(v_hi, 1)

            def ct_part(act, f, j):
                act.wait_ge(ct_rdy, 2 * f + j + 1)
                af(cth[:, :, 256 * j:256 * j + 256], bank[CT_BANK[j]][:, :].rearrange("p (k c) -> p k c", k=KD),
                   ACT.Copy).then_inc(ct_hi, 1)

            def squares(act, f, j):
                act.wait_ge(y_dn, 2 * f + j + 1)
                for t in range(CG * j, CG * j + CG):
                    if t > 0:
                        act.wait_ge(sq_dn, 4 * f + t)
                    af(ysq[:, :], y[:, t, :], ACT.Square, scale=D ** -0.5, accum_out=yms[:, t:t + 1]).then_inc(sq_dn, 1)

            def a1_part(act, g, j):
                act.wait_ge(a1_rdy, 2 * g + j + 1)
                for e in range(CG * j, CG * j + CG):
                    af(a1h[:, e, :], bank[A1_BANK[j]][:, D * (e % CG):D * (e % CG) + D], ACT.Copy,
                       scale=be[:, e:e + 1]).then_inc(a1_hi, 1)

            def x2_part(act, f, j):
                act.wait_ge(yrs_st, 8 * f + 4 * j + 4)
                for t in range(CG * j, CG * j + CG):
                    af(x2[:, t, :], x1[:, t, :], ACT.Identity, bias=ynb[:, t:t + 1],
                       scale=yrs[:, t:t + 1]).then_inc(x2_dn, 1)

            def body(act, g, conv, ffn, late, prep):
                f = g - 1
                if conv:
                    if ffn:
                        act.wait_ge(be_max, g)
                    for k in range(CT):
                        act.wait_ge(ht_rdy, 4 * g + k + 1)
                        af(ht16[:, k, :], bank[HT_BANK[k]][:, 0:256].bitcast(F16), ACT.Copy,
                           accum_out=deg[:, k:k + 1]).then_inc(ht_cp, 1)
                    act.wait_ge(be_dn, g + 1)
                    a1_part(act, g, 0)
                if ffn:
                    x2_part(act, f, 0)
                if conv:
                    a1_part(act, g, 1)
                if ffn:
                    x2_part(act, f, 1)
                if ffn:
                    for j in range(2):
                        act.wait_ge(xt_rdy, 2 * f + j + 1)
                        af(xth[:, :, 256 * j:256 * j + 256],
                           bank[XT_BANK[j]][:, :].rearrange("p (k c) -> p k c", k=KD),
                           ACT.Copy, scale=XS).then_inc(xt_hi, 1)
                if conv:
                    for k in range(KD):
                        act.wait_ge(a2_rdy, 2 * g + k + 1)
                        af(a2h[:, k, :], bank[A2_BANK[k]][:, :], ACT.Copy, scale=A2S).then_inc(a2_hi, 1)
                if ffn:
                    expert(act, f, 0)
                if prep:
                    prep_x(g + 1, (0, 1))
                if ffn:
                    act.wait_ge(arg_dn, f + 1)
                    af(th[:, :, :], arg[:, :, :], ACT.Tanh).then_inc(th_dn, 1)
                    expert(act, f, 1)
                if prep:
                    prep_x(g + 1, (2, 3))
                    prep_x_hi(g + 1)
                if conv:
                    relu(act, g, 0)
                    relu(act, g, 1)
                    relu(act, g, 2)
                    norm_h(act, g, 0)
                    relu(act, g, 3)
                if ffn:
                    expert(act, f, 2)
                if conv:
                    norm_h(act, g, 1)
                if ffn:
                    expert(act, f, 3)
                if conv:
                    norm_h(act, g, 2)
                if ffn:
                    expert(act, f, 4)
                if conv:
                    norm_h(act, g, 3)
                if ffn:
                    expert(act, f, 5)
                if conv:
                    hnt_part(act, g, 0)
                    hnt_part(act, g, 1)
                if ffn:
                    expert(act, f, 6)
                    expert(act, f, 7)
                if conv:
                    hnt_part(act, g, 2)
                    v_part(act, g, 0)
                    hnt_part(act, g, 3)
                if ffn:
                    ct_part(act, f, 0)
                if conv:
                    v_part(act, g, 1)
                if ffn:
                    ct_part(act, f, 1)
                    squares(act, f, 0)
                if conv:
                    for e in range(CT):
                        if e % CG == 0:
                            act.wait_ge(u_rdy, 2 * g + e // CG + 1)
                        af(uh[:, e, :], bank[U_BANK[e // CG]][:, D * (e % CG):D * (e % CG) + D], ACT.Copy,
                           scale=be[:, e:e + 1]).then_inc(u_hi, 1)
                if ffn:
                    squares(act, f, 1)
            steps(act, body)

        @block.vector
        def _(dve):
            v = nc.vector
            TT, TS, STT = v.tensor_tensor, v.tensor_scalar, v.scalar_tensor_tensor
            own = sem("dve_setup")
            count = [0]

            def done(ins):
                count[0] += 1
                ins.then_inc(own, 1)
                dve.wait_ge(own, count[0])

            def flat(t):
                return t[:, :, :, :].rearrange("p t e j -> p (t e j)")

            def prep_h(g, again=True):
                dve.wait_ge(adj_in, 16 * g + 16)
                if again:
                    dve.wait_ge(u_rdy, 2 * g)
                TS(h16[:, :, :], adjin[:, :, :], 0.0, None, ALU.not_equal).then_inc(h_made, 1)

            def prep_x_stats(g):
                dve.wait_ge(x_in, 16 * g + 16)
                for t in range(CT):
                    v.bn_stats(xbn[:, t, :], xin[:, t, :]).then_inc(xbn_dn, 1)

            def prep_x_aggr(g, again=True):
                dve.wait_ge(xbn_dn, 4 * g + 4)
                if again:
                    dve.wait_ge(xrs_st, 4 * g)
                v.memset(spare[:, :], 0.0)
                for t in range(CT):
                    ins = v.bn_aggr(xmv[:, t, :], xbn[:, t, :])
                ins.then_inc(xstat, 1)

            def prep_x_lo(g):
                dve.wait_ge(xs_hi, g + 1)
                STT(xsl[:, :, :], xn[:, :, :], XS, xsh[:, :, :], ALU.mult, ALU.subtract).then_inc(xs_lo, 1)

            prep_h(0, again=False)
            prep_x_stats(0)
            prep_x_aggr(0, again=False)
            done(v.memset(mags[:, :], 0.0))
            done(v.memset(ones[:, :], 1.0))
            done(v.memset(ebias[:, :], 0.0))
            done(v.memset(vbias[:, :], 0.0))
            dve.wait_ge(w_in, 16 * NWEIGHTS)
            for k in range(KH):
                done(TS(w2g[:, k, :], w2f[:, k, :], gam[:, k:k + 1], None, ALU.mult))
            for t in range(1, CT):
                done(v.tensor_copy(rbb[:, t, :], rbb[:, 0, :]))

            def magnitude(col, src, rows, n, scale):
                done(STT(absbuf[0:rows, 0:n], src, -1.0, src, ALU.mult, ALU.max))
                done(v.reduce_max(mags[0:rows, col:col + 1], absbuf[0:rows, 0:n], X))
                if scale != 1.0:
                    done(TS(mags[0:rows, col:col + 1], mags[0:rows, col:col + 1], scale, None, ALU.mult))

            magnitude(0, w1f[:, :, :].rearrange("p k n -> p (k n)"), P, KD * DH, 1.0)
            magnitude(1, w2g[:, :, :].rearrange("p k n -> p (k n)"), P, KH * D, 1.0)
            magnitude(2, ewf[:, :, :].rearrange("p k n -> p (k n)"), P, KD * NE * D, 1.0)
            magnitude(3, owf[:, :, :].rearrange("p k n -> p (k n)"), P, KD * D, 1.0)
            magnitude(4, rwf[:, :, :].rearrange("p k n -> p (k n)"), P, KD * NE, 1.0)
            magnitude(5, ebrow[0:1, :], 1, NE * D, 1.0 / D)
            dve.wait_ge(c_pe, 1)
            done(v.tensor_copy(bwrow[0:1, :], bank[0][0:1, 0:D]))
            magnitude(6, bwrow[0:1, :], 1, D, 1.0 / DH)
            v.memset(mags[:, 7:8], 0.0).then_inc(c_dve, 1)
            done(v.tensor_copy(wparts[:, :, :, 0], wf[:, :, :]))
            done(TT(wr1[:, :, :], wf[:, :, :], wparts[:, :, :, 0], ALU.subtract))
            done(v.tensor_copy(wparts[:, :, :, 1], wr1[:, :, :]))
            done(TT(wr2[:, :, :], wr1[:, :, :], wparts[:, :, :, 1], ALU.subtract))
            v.tensor_copy(wparts[:, :, :, 2], wr2[:, :, :]).then_inc(c_dve, 1)
            dve.wait_ge(c_pool, 11)
            done(TT(pmax[:, 1:2], pmax[:, 1:2], pmax[:, 6:7], ALU.max))
            done(TT(pmax[:, 2:3], pmax[:, 2:3], pmax[:, 5:6], ALU.max))
            done(TS(pmax[:, :], pmax[:, :], 1e-30, 1e30, ALU.max, ALU.min))
            done(TS(pw[:, :].bitcast(I32), pmax[:, :].bitcast(I32), 0x7F800000, None, ALU.bitwise_and))
            done(v.reciprocal(ipw[:, :], pw[:, :]))
            done(TS(wsc[:, :], ipw[:, :], WS, None, ALU.mult))
            done(TS(ksc[:, 0:1], pw[:, 0:1], 1.0 / (XS * A2S * WS), None, ALU.mult))
            done(TS(ksc[:, 1:2], pw[:, 1:2], 1.0 / (HS * WS * VS), None, ALU.mult))
            done(TS(ksc[:, 2:3], pw[:, 2:3], 1.0 / (XS * WS), None, ALU.mult))
            done(TS(ksc[:, 3:4], pw[:, 3:4], 2.0 ** -5 / WS, pw[:, 2:3], ALU.mult, ALU.mult))
            done(TS(ksc[:, 4:5], pw[:, 4:5], 1.0 / (XS * WS), None, ALU.mult))
            done(TS(ksc[:, 5:6], ipw[:, 2:3], 2.0 ** 4, None, ALU.mult))
            v.tensor_copy(ksc[:, 6:7], ksc[:, 5:6]).then_inc(c_dve, 1)
            for col, n, src, scale, dst in ((1, D, bwrow, HS, vbias), (2, NE * D, ebrow, XS, ebias)):
                done(TS(brow[0:1, 0:n], src[0:1, 0:n], wsc[0:1, col:col + 1], scale, ALU.mult, ALU.mult))
                for part in range(3):
                    row = dst[32 * part:32 * part + 1, 0:n]
                    done(v.tensor_copy(row, brow[0:1, 0:n]))
                    if part < 2:
                        done(v.tensor_copy(absbuf[0:1, 0:n], row))
                        done(TT(brow[0:1, 0:n], brow[0:1, 0:n], absbuf[0:1, 0:n], ALU.subtract))
            dve.wait_ge(c_act, 6)
            for i, (full, hi, lo) in enumerate(((w1f, w1h, w1l), (w2g, w2h, w2l), (ewf, ewh, ewl),
                                                (owf, owh, owl), (rwf, rwh, rwl))):
                ins = STT(lo[:, :, :], full[:, :, :], wsc[:, i:i + 1], hi[:, :, :], ALU.mult, ALU.subtract)
                if i < 4:
                    done(ins)
            ins.then_inc(c_dve, 1)
            prep_x_lo(0)

            def combine(f, t, e):
                src = silu[:, (2 * t + e // 2) % 4, D * (e % 2):D * (e % 2) + D]
                m = mask[:, t, e:e + 1]
                if e % 2 == 0:
                    dve.wait_ge(silu_dn, 8 * f + 2 * t + e // 2 + 1)
                if e == 0:
                    TS(comb[:, t, :], src, m, None, ALU.mult).then_inc(comb_st, 1)
                else:
                    dve.wait_ge(comb_st, 16 * f + 4 * t + e)
                    STT(comb[:, t, :], src, m, comb[:, t, :], ALU.mult, ALU.add).then_inc(comb_st, 1)

            def z_part(g, t):
                dve.wait_ge(a3_rdy, 4 * g + t + 1)
                STT(z[:, t, :], bank[A3_BANK[t]][:, :], dna[:, t:t + 1], b1b[:, :], ALU.mult, ALU.add).then_inc(z_dn, 1)

            def h_stats(g, t):
                dve.wait_ge(relu_dn, 4 * g + t + 1)
                v.bn_stats(hbn[:, t, :], r[:, t, :]).then_inc(hbn_dn, 1)

            def h_aggr(g, t):
                v.bn_aggr(hmv[:, t, :], hbn[:, t, :]).then_inc(hstat, 1)

            def hnt_part(g, t):
                dve.wait_ge(hnt_hi, 4 * g + t + 1)
                STT(hntl[:, t, :], bank[HNT_BANK[t]][:, :], HS, hnth[:, t, :], ALU.mult, ALU.subtract).then_inc(hnt_lo, 1)

            def v_part(g, j):
                dve.wait_ge(v_hi, 2 * g + j + 1)
                s = slice(CG * j, CG * j + CG)
                STT(vl[:, s, :], bank[V_BANK[j]][:, :].rearrange("p (t d) -> p t d", t=CG), VS, vh[:, s, :],
                    ALU.mult, ALU.subtract).then_inc(v_lo, 1)

            def ct_part(f, j):
                dve.wait_ge(ct_hi, 2 * f + j + 1)
                s = slice(256 * j, 256 * j + 256)
                TT(ctl[:, :, s], bank[CT_BANK[j]][:, :].rearrange("p (k c) -> p k c", k=KD), cth[:, :, s],
                   ALU.subtract).then_inc(ct_lo, 1)

            def y_part(f, j):
                dve.wait_ge(o_rdy, 2 * f + j + 1)
                if j == 0:
                    dve.wait_ge(x2o_dn, f + 1)
                s = slice(CG * j, CG * j + CG)
                STT(y[:, s, :], bank[O_BANK[j]][:, :].rearrange("p (t d) -> p t d", t=CG), ksc[:, 3:4], x2o[:, s, :],
                    ALU.mult, ALU.add).then_inc(y_dn, 1)

            def a1_part(g, j):
                dve.wait_ge(a1_hi, 4 * g + CG * j + CG)
                for e in range(CG * j, CG * j + CG):
                    STT(a1l[:, e, :], bank[A1_BANK[j]][:, D * (e % CG):D * (e % CG) + D], be[:, e:e + 1], a1h[:, e, :],
                        ALU.mult, ALU.subtract).then_inc(a1_lo, 1)

            def d_vector(g):
                dve.wait_ge(d_rdy, g + 1)
                v.reduce_sum(dsum[:, :], bank[D_BANK][:, 0:CT * 4].rearrange("p (t w) -> p t w", w=4)[:, :, 0:3],
                             X).then_inc(d_step, 1)
                dve.wait_ge(d_step, 6 * g + 1)
                TS(dclip[:, :], dsum[:, :], 1.2e-38, None, ALU.max).then_inc(d_step, 1)
                dve.wait_ge(d_step, 6 * g + 2)
                v.reciprocal(drec[:, :], dclip[:, :]).then_inc(d_step, 1)
                dve.wait_ge(d_step, 6 * g + 3)
                STT(dn[:, :], dsum[:, :], 0.0, drec[:, :], ALU.is_gt, ALU.mult).then_inc(d_step, 1)
                dve.wait_ge(d_step, 6 * g + 4)
                TS(dna[:, :], dn[:, :], ksc[:, 0:1], None, ALU.mult).then_inc(d_step, 1)
                TS(dnb[:, :], dn[:, :], ksc[:, 1:2], None, ALU.mult).then_inc(d_step, 1)

            def route(f):
                dve.wait_ge(lg_rdy, f + 1)
                STT(lg[:, :, :], bank[R_BANK][:, 0:CT * NE].rearrange("p (t e) -> p t e", e=NE), ksc[:, 4:5],
                    rbb[:, :, :], ALU.mult, ALU.add).then_inc(lg_dn, 1)
                dve.wait_ge(lg_dn, f + 1)
                TT(ldf[:, :, :, :], lg[:, :, :].unsqueeze(2).to_broadcast([P, CT, NE, NE]),
                   lg[:, :, :].unsqueeze(3).to_broadcast([P, CT, NE, NE]), ALU.subtract).then_inc(r_step, 1)
                dve.wait_ge(r_step, 8 * f + 1)
                STT(flat(tie), flat(ldf), 0.0, flat(tri), ALU.is_ge, ALU.mult).then_inc(r_step, 1)
                dve.wait_ge(r_step, 8 * f + 2)
                STT(flat(beat), flat(ldf), 0.0, flat(tie), ALU.is_gt, ALU.max).then_inc(r_step, 1)
                dve.wait_ge(r_step, 8 * f + 3)
                v.reduce_sum(rank[:, :, :], beat[:, :, :, :], X).then_inc(r_step, 1)
                dve.wait_ge(r_step, 8 * f + 4)
                STT(lsel[:, :, :], rank[:, :, :], 1.5, lg[:, :, :], ALU.is_lt, ALU.mult).then_inc(r_step, 1)
                dve.wait_ge(r_step, 8 * f + 5)
                v.reduce_sum(lsum[:, :], lsel[:, :, :], X).then_inc(r_step, 1)
                dve.wait_ge(r_step, 8 * f + 6)
                STT(arg[:, :, :], lsum[:, :].unsqueeze(2).to_broadcast([P, CT, NE]), -0.5, lg[:, :, :],
                    ALU.mult, ALU.add).then_inc(arg_dn, 1)

            def make_mask(f):
                dve.wait_ge(th_dn, f + 1)
                TS(wt[:, :, :], th[:, :, :], ksc[:, 5:6], ksc[:, 6:7], ALU.mult, ALU.add).then_inc(r_step, 1)
                dve.wait_ge(r_step, 8 * f + 7)
                STT(mask[:, :, :], rank[:, :, :], 1.5, wt[:, :, :], ALU.is_lt, ALU.mult).then_inc(r_step, 1)
                dve.wait_ge(r_step, 8 * f + 8)

            def finish(q, tiles):
                dve.wait_ge(rr_st, 2 * q + 2)
                for t in tiles:
                    STT(yf[:, t, :], y[:, t, :], yrr[:, t:t + 1], nwb[:, :], ALU.mult, ALU.mult).then_inc(yf_dn, 1)

            def body(dve, g, conv, ffn, late, prep):
                f, q = g - 1, g - 2
                if conv:
                    dve.wait_ge(ht_cp, 4 * g + 4)
                    TS(dmax[:, :], deg[:, :], 1.0, None, ALU.max).then_inc(be_max, 1)
                    dve.wait_ge(be_max, g + 1)
                    v.reciprocal(be[:, :], dmax[:, :]).then_inc(be_dn, 1)
                if late:
                    finish(q, (0, 1))
                if conv:
                    a1_part(g, 0)
                if late:
                    finish(q, (2, 3))
                if conv:
                    a1_part(g, 1)
                if prep:
                    prep_x_stats(g + 1)
                if ffn:
                    for j in range(2):
                        dve.wait_ge(xt_hi, 2 * f + j + 1)
                        s = slice(256 * j, 256 * j + 256)
                        STT(xtl[:, :, s], bank[XT_BANK[j]][:, :].rearrange("p (k c) -> p k c", k=KD), XS,
                            xth[:, :, s], ALU.mult, ALU.subtract).then_inc(xt_lo, 1)
                if conv:
                    d_vector(g)
                if prep:
                    prep_x_aggr(g + 1)
                if conv:
                    dve.wait_ge(a2_hi, 2 * g + 1)
                    STT(a2l[:, 0, :], bank[A2_BANK[0]][:, :], A2S, a2h[:, 0, :], ALU.mult,
                        ALU.subtract).then_inc(a2_lo, 1)
                    dve.wait_ge(a2_hi, 2 * g + 2)
                    STT(a2l[:, 1, :], bank[A2_BANK[1]][:, :], A2S, a2h[:, 1, :], ALU.mult,
                        ALU.subtract).then_inc(a2_lo, 1)
                if ffn:
                    route(f)
                    make_mask(f)
                    combine(f, 0, 0)
                    combine(f, 0, 1)
                if conv:
                    dve.wait_ge(d_step, 6 * g + 6)
                    z_part(g, 0)
                if ffn:
                    combine(f, 0, 2)
                if conv:
                    z_part(g, 1)
                if ffn:
                    combine(f, 0, 3)
                if conv:
                    h_stats(g, 0)
                    dve.wait_ge(hbn_dn, 4 * g + 1)
                    z_part(g, 2)
                    h_aggr(g, 0)
                    h_stats(g, 1)
                    dve.wait_ge(hbn_dn, 4 * g + 2)
                    z_part(g, 3)
                    h_aggr(g, 1)
                    h_stats(g, 2)
                if ffn:
                    combine(f, 1, 0)
                    combine(f, 1, 1)
                if conv:
                    dve.wait_ge(hbn_dn, 4 * g + 3)
                    h_stats(g, 3)
                    h_aggr(g, 2)
                    dve.wait_ge(hbn_dn, 4 * g + 4)
                    v.memset(spare[:, :], 0.0)
                    h_aggr(g, 3)
                if ffn:
                    combine(f, 1, 2)
                    combine(f, 1, 3)
                    combine(f, 2, 0)
                    combine(f, 2, 1)
                    combine(f, 2, 2)
                    combine(f, 2, 3)
                if conv:
                    hnt_part(g, 0)
                if ffn:
                    combine(f, 3, 0)
                    combine(f, 3, 1)
                if conv:
                    hnt_part(g, 1)
                if ffn:
                    combine(f, 3, 2)
                    combine(f, 3, 3)
                if conv:
                    hnt_part(g, 2)
                    v_part(g, 0)
                    hnt_part(g, 3)
                if ffn:
                    ct_part(f, 0)
                if prep:
                    prep_x_lo(g + 1)
                if conv:
                    v_part(g, 1)
                if ffn:
                    ct_part(f, 1)
                    y_part(f, 0)
                    if late and not prep:
                        dve.wait_ge(out_rdy, 2 * f)
                    v.tensor_copy(x1k[:, :, :], x1[:, :, :]).then_inc(x1_kept, 1)
                if conv:
                    for e in range(CT):
                        if e % CG == 0:
                            dve.wait_ge(u_hi, 4 * g + e + CG)
                        STT(ul[:, e, :], bank[U_BANK[e // CG]][:, D * (e % CG):D * (e % CG) + D],
                            be[:, e:e + 1], uh[:, e, :], ALU.mult, ALU.subtract).then_inc(u_lo, 1)
                if ffn:
                    y_part(f, 1)
                if prep:
                    prep_h(g + 1)
                if conv:
                    dve.wait_ge(xb_dn, g + 1)
                    if ffn:
                        dve.wait_ge(x1_kept, f + 1)
                    for j in range(2):
                        dve.wait_ge(b3_rdy, 2 * g + j + 1)
                        for t in range(CG * j, CG * j + CG):
                            STT(x1[:, t, :], bank[B3_BANK[j]][:, D * (t % CG):D * (t % CG) + D],
                                dnb[:, t:t + 1], xb[:, t, :], ALU.mult, ALU.add).then_inc(x1_dn, 1)
                        for t in range(CG * j, CG * j + CG):
                            dve.wait_ge(x1_dn, 4 * g + t + 1)
                            v.bn_stats(ybn[:, t, :], x1[:, t, :]).then_inc(ybn_dn, 1)
                        dve.wait_ge(ybn_dn, 4 * g + CG * j + CG)
                        v.memset(spare[:, :], 0.0)
                        for t in range(CG * j, CG * j + CG):
                            ins = v.bn_aggr(ymv[:, t, :], ybn[:, t, :])
                        ins.then_inc(ystat, 1)
            steps(dve, body)

        @block.tensor
        def _(pe):
            mm = nc.tensor.matmul

            def three(outp, lh, ll, rh, rl, first, last):
                mm(outp, lh, rh, start=first, stop=False)
                mm(outp, lh, rl, start=False, stop=False)
                return mm(outp, ll, rh, start=False, stop=last)

            pe.wait_ge(w_in, 16 * NWEIGHTS)
            for k in range(KH):
                ins = mm(bank[0][0:1, 0:D], bet[:, k:k + 1], w2f[:, k, :], start=(k == 0), stop=(k == KH - 1))
            ins.then_inc(c_pe, 1)

            def experts(f, t):
                for p in range(2):
                    i = 2 * t + p
                    b = bank[E_BANK[i]][:, :]
                    if i == 2:
                        pe.wait_ge(lg_dn, f + 1)
                    if i >= 3:
                        pe.wait_ge(silu_dn, 8 * f + i - 2)
                    mm(b, ones[:, :], ebias[:, 512 * p:512 * p + 512], start=True, stop=False)
                    for k in range(KD):
                        ins = three(b, xth[:, k, P * t:P * t + P], xtl[:, k, P * t:P * t + P],
                                    ewh[:, k, 512 * p:512 * p + 512], ewl[:, k, 512 * p:512 * p + 512], False, k == KD - 1)
                    ins.then_inc(e_rdy, 1)

            def transposed_h(g, t):
                pe.wait_ge(hn_dn, 4 * g + t + 1)
                if t >= 2:
                    pe.wait_ge(hnt_lo, 4 * g + t - 1)
                for k in range(KH):
                    ins = nc.tensor.transpose(bank[HNT_BANK[t]][:, P * k:P * k + P], hn[:, t, P * k:P * k + P], ident[:, :])
                ins.then_inc(hnt_rdy, 1)

            def v_tile(g, t):
                pe.wait_ge(hnt_lo, 4 * g + t + 1)
                if t == 0:
                    pe.wait_ge(z_dn, 4 * g + 4)
                b = bank[V_BANK[t // CG]][:, D * (t % CG):D * (t % CG) + D]
                mm(b, ones[:, :], vbias[:, :], start=True, stop=False)
                for k in range(KH):
                    ins = three(b, hnth[:, t, P * k:P * k + P], hntl[:, t, P * k:P * k + P], w2h[:, k, :], w2l[:, k, :],
                                False, k == KH - 1)
                if t % CG == CG - 1:
                    ins.then_inc(v_rdy, 1)

            def transposed_comb(f, j):
                if j == 0:
                    pe.wait_ge(silu_dn, 8 * f + 6)
                pe.wait_ge(comb_st, 16 * f + 4 * (CG * j + CG))
                for k in range(KD):
                    for t in range(CG):
                        ins = nc.tensor.transpose(bank[CT_BANK[j]][:, 256 * k + P * t:256 * k + P * t + P],
                                                  comb[:, CG * j + t, P * k:P * k + P], ident[:, :])
                ins.then_inc(ct_rdy, 1)

            def out_product(f, j):
                pe.wait_ge(ct_lo, 2 * f + j + 1)
                for t in range(CG * j, CG * j + CG):
                    b = bank[O_BANK[j]][:, D * (t % CG):D * (t % CG) + D]
                    for k in range(KD):
                        ins = three(b, cth[:, k, P * t:P * t + P], ctl[:, k, P * t:P * t + P], owh[:, k, :], owl[:, k, :],
                                    k == 0, k == KD - 1)
                ins.then_inc(o_rdy, 1)

            def incidence(g, banks, weights, hi, lo, s_lo, per, s_rdy):
                def part(e, ks):
                    b = bank[banks[e // CG]][:, D * (e % CG):D * (e % CG) + D]
                    for k in ks:
                        mm(b, weights[:, k, P * e:P * e + P], hi[:, k, :], start=(k == 0), stop=False)
                        ins = mm(b, weights[:, k, P * e:P * e + P], lo[:, k, :], start=False, stop=(k == CT - 1))
                    return ins

                pe.wait_ge(s_lo, per * g + per // 2)
                part(0, (0, 1))
                part(CG, (0, 1))
                pe.wait_ge(s_lo, per * g + per)
                part(0, (2, 3))
                part(1, range(CT)).then_inc(s_rdy, 1)
                part(CG, (2, 3))
                part(CG + 1, range(CT)).then_inc(s_rdy, 1)

            def a2_half(g, half):
                pe.wait_ge(a1_lo, 4 * g + CG * half + CG)
                for d in range(KD):
                    if half == 0:
                        pe.wait_ge(ht_cp, 4 * g + 3 + d)
                    for k in range(CG * half, CG * half + CG):
                        mm(bank[A2_BANK[d]][:, :], a1h[:, k, P * d:P * d + P], ht16[:, k, :],
                           start=(k == 0), stop=False)
                        ins = mm(bank[A2_BANK[d]][:, :], a1l[:, k, P * d:P * d + P], ht16[:, k, :],
                                 start=False, stop=(k == CT - 1))
                    if half == 1:
                        ins.then_inc(a2_rdy, 1)

            def body(pe, g, conv, ffn, late, prep):
                f = g - 1
                if conv:
                    pe.wait_ge(h_made, g + 1)
                    for k in range(CT):
                        if ffn:
                            if k == 0:
                                pe.wait_ge(hnt_lo, 4 * g)
                            elif k == 1:
                                pe.wait_ge(u_lo, 4 * (g - 1) + 2)
                            elif k == 2:
                                pe.wait_ge(u_lo, 4 * g)
                            else:
                                pe.wait_ge(x1_dn, 4 * (g - 1) + 2)
                        for c in range(CT):
                            ins = nc.tensor.transpose(bank[HT_BANK[k]][:, 0:256].bitcast(F16)[:, P * c:P * c + P],
                                                      h16[:, c, P * k:P * k + P], ident16[:, :])
                        ins.then_inc(ht_rdy, 1)
                    pe.wait_ge(xs_lo, g + 1)
                    for e in range(CT):
                        if e % CG == 0:
                            pe.wait_ge(ht_cp, 4 * g + e // CG + 1)
                        b = bank[A1_BANK[e // CG]][:, D * (e % CG):D * (e % CG) + D]
                        for k in range(CT):
                            mm(b, h16[:, k, P * e:P * e + P], xsh[:, k, :], start=(k == 0), stop=False)
                            ins = mm(b, h16[:, k, P * e:P * e + P], xsl[:, k, :], start=False, stop=(k == CT - 1))
                        if e % CG == CG - 1:
                            ins.then_inc(a1_rdy, 1)
                    pe.wait_ge(ht_cp, 4 * g + 4)
                    pe.wait_ge(w_cur, g + 1)
                    if ffn:
                        pe.wait_ge(x1_dn, 4 * g)
                    for t in range(CT):
                        for k in range(CT):
                            ins = mm(bank[D_BANK][:, 4 * t:4 * t + 3], ht16[:, k, P * t:P * t + P], wcur[:, k, :],
                                     start=(k == 0), stop=(k == CT - 1))
                    ins.then_inc(d_rdy, 1)
                if conv:
                    a2_half(g, 0)
                if ffn:
                    for j in range(2):
                        pe.wait_ge(x2_dn, 4 * f + CG * j + CG)
                        for k in range(KD):
                            for t in range(CG):
                                ins = nc.tensor.transpose(bank[XT_BANK[j]][:, 256 * k + P * t:256 * k + P * t + P],
                                                          x2[:, CG * j + t, P * k:P * k + P], ident[:, :])
                        ins.then_inc(xt_rdy, 1)
                if conv:
                    a2_half(g, 1)
                if ffn:
                    pe.wait_ge(xt_lo, 2 * f + 2)
                    for t in range(CT):
                        for k in range(KD):
                            ins = three(bank[R_BANK][:, NE * t:NE * t + NE], xth[:, k, P * t:P * t + P],
                                        xtl[:, k, P * t:P * t + P], rwh[:, k, :], rwl[:, k, :], k == 0, k == KD - 1)
                    ins.then_inc(lg_rdy, 1)
                    experts(f, 0)
                if conv:
                    pe.wait_ge(a2_lo, 2 * g + 2)
                    for t in range(CT):
                        for k in range(KD):
                            ins = three(bank[A3_BANK[t]][:, :], a2h[:, k, P * t:P * t + P], a2l[:, k, P * t:P * t + P],
                                        w1h[:, k, :], w1l[:, k, :], k == 0, k == KD - 1)
                        ins.then_inc(a3_rdy, 1)
                if ffn:
                    experts(f, 1)
                    experts(f, 2)
                if conv:
                    transposed_h(g, 0)
                    transposed_h(g, 1)
                if ffn:
                    experts(f, 3)
                if conv:
                    v_tile(g, 0)
                    transposed_h(g, 2)
                    v_tile(g, 1)
                    transposed_h(g, 3)
                    v_tile(g, 2)
                if ffn:
                    transposed_comb(f, 0)
                if conv:
                    v_tile(g, 3)
                if ffn:
                    transposed_comb(f, 1)
                    out_product(f, 0)
                if conv:
                    incidence(g, U_BANK, h16, vh, vl, v_lo, 2, u_rdy)
                if ffn:
                    out_product(f, 1)
                if conv:
                    incidence(g, B3_BANK, ht16, uh, ul, u_lo, 4, b3_rdy)

            pe.wait_ge(c_pool, 10)
            pe.wait_ge(c_dve, 4)
            steps(pe, body)


def kernel(x, adj, L0_gnn_W1, L0_gnn_b1, L0_gnn_gamma, L0_gnn_beta, L0_gnn_W2, L0_gnn_b2, L0_ffn_router_w,
           L0_ffn_router_b, L0_ffn_expert_w, L0_ffn_expert_b, L0_ffn_out_w, L0_ffn_out_b, L0_ffn_norm_w):
    import numpy as np
    import concourse.bacc as bacc
    from concourse.bass_utils import run_bass_kernel_spmd

    def arr(a):
        return np.ascontiguousarray(a)

    x, adj = np.asarray(x), np.asarray(adj)
    n, c, d = x.shape
    dh = L0_gnn_b1.shape[0]
    ne = L0_ffn_expert_w.shape[0]
    arrays = {
        "x": arr(x),
        "adj": arr(adj),
        "wrow": arr(adj[:, 0, :].reshape(n, c // P, P).transpose(2, 0, 1)),
        "w1t": arr(np.asarray(L0_gnn_W1).T),
        "b1": arr(np.asarray(L0_gnn_b1).reshape(1, dh)),
        "gamma": arr(np.asarray(L0_gnn_gamma).reshape(dh // P, P).T),
        "beta": arr(np.asarray(L0_gnn_beta).reshape(dh // P, P).T),
        "w2t": arr(np.asarray(L0_gnn_W2).T),
        "b2": arr(np.asarray(L0_gnn_b2).reshape(1, d)),
        "rw": arr(L0_ffn_router_w),
        "rb": arr(np.asarray(L0_ffn_router_b).reshape(1, ne)),
        "ew": arr(np.asarray(L0_ffn_expert_w).transpose(1, 0, 2)),
        "eb": arr(np.asarray(L0_ffn_expert_b).reshape(1, ne * d)),
        "ow": arr(L0_ffn_out_w),
        "ob": arr(np.asarray(L0_ffn_out_b).reshape(1, d)),
        "nw": arr(np.asarray(L0_ffn_norm_w).reshape(1, d)),
    }
    nc = bacc.Bacc("TRN2", target_bir_lowering=False, num_devices=1)
    args = [nc.dram_tensor(k, a.shape, mybir.dt.from_np(a.dtype), kind="ExternalInput").ap() for k, a in arrays.items()]
    res = nc.dram_tensor("out", (n, c, d), F32, kind="ExternalOutput").ap()
    build(nc, *args, res)
    got = run_bass_kernel_spmd(nc, [arrays], core_ids=[0])
    return got.results[0]["out"]
```

```python
from contextlib import ExitStack

import concourse.bass as bass
from concourse import mybir

ALU = mybir.AluOpType
ACT = mybir.ActivationFunctionType
F32 = mybir.dt.float32
F16 = mybir.dt.float16
BF16 = mybir.dt.bfloat16
I32 = mybir.dt.int32
X = mybir.AxisListType.X
RMAX = bass.bass_isa.ReduceOp.max

P = 128
EPS_LN = 1e-5
EPS_RMS = 1e-6

XS = 2.0 ** 11
A2S = 2.0 ** -9
HS = 2.0 ** 10
WS = 2.0 ** 13
VS = 2.0 ** -19


def build(nc, x, adj, wrow, w1t, b1, gamma, beta, w2t, b2, rw, rb, ew, eb, ow, ob, nw, out):
    N, C, D = x.shape
    DH = w1t.shape[1]
    NE = ew.shape[1]
    CT, KD, KH = C // P, D // P, DH // P
    CG = 2
    assert (C, D, DH, NE) == (512, 256, 512, 4)

    with ExitStack() as ctx:
        def sb(name, shape, dt):
            return ctx.enter_context(nc.sbuf_tensor(name, shape, dt))

        def sem(name):
            return ctx.enter_context(nc.semaphore(name))

        bank = [ctx.enter_context(nc.psum_tensor(f"bank{i}", [P, 512], F32)) for i in range(8)]
        HT_BANK, A1_BANK, D_BANK, A2_BANK = (0, 3, 4, 1), (0, 3), 2, (4, 1)
        A3_BANK, HNT_BANK, V_BANK, U_BANK, B3_BANK = (0, 3, 4, 1), (2, 0, 2, 0), (1, 2), (3, 4), (1, 2)
        XT_BANK, R_BANK, E_BANK, O_BANK = (5, 6), 7, (5, 6, 7, 5, 6, 7, 5, 6), (6, 7)
        MT_BANK, MB_BANK = 2, (3, 4, 3, 4)

        w1f = sb("w1f", [P, KD, DH], F32)
        w2f = sb("w2f", [P, KH, D], F32)
        w2g = sb("w2g", [P, KH, D], F32)
        ewf = sb("ewf", [P, KD, NE * D], F32)
        owf = sb("owf", [P, KD, D], F32)
        rwf = sb("rwf", [P, KD, NE], F32)
        w1h, w1l = sb("w1h", [P, KD, DH], F16), sb("w1l", [P, KD, DH], F16)
        w2h, w2l = sb("w2h", [P, KH, D], F16), sb("w2l", [P, KH, D], F16)
        ewh, ewl = sb("ewh", [P, KD, NE * D], F16), sb("ewl", [P, KD, NE * D], F16)
        owh, owl = sb("owh", [P, KD, D], F16), sb("owl", [P, KD, D], F16)
        rwh, rwl = sb("rwh", [P, KD, NE], F16), sb("rwl", [P, KD, NE], F16)
        gam, bet = sb("gam", [P, KH], F32), sb("bet", [P, KH], F32)
        b1b = sb("b1b", [P, DH], F32)
        b2b, obb = sb("b2b", [P, D], F32), sb("obb", [P, D], F32)
        nwb = sb("nwb", [P, D], F32)
        rbb = sb("rbb", [P, CT, NE], F32)
        ebcol = sb("ebcol", [P, NE * D // P], F32)
        bwcol = sb("bwcol", [P, D // P], F32)
        babs = sb("babs", [P, NE * D // P], F32)
        bval = sb("bval", [P, NE * D // P], F32)
        vbparts = sb("vbparts", [P, 3, D // P], BF16)
        vbias = sb("vbias", [P, D], BF16)
        ones = sb("ones", [P, P], BF16)
        absbuf = sb("absbuf", [P, 2, 1024], F32)
        W1, W2, VB, EX, EB, OW, RW = range(7)
        mags = sb("mags", [P, 8], F32)
        pmax = sb("pmax", [P, 8], F32)
        pw = sb("pw", [P, 8], F32)
        ipw = sb("ipw", [P, 8], F32)
        wsc = sb("wsc", [P, 8], F32)
        ksc = sb("ksc", [P, 8], F32)
        ident = sb("ident", [P, P], F32)
        ident16 = sb("ident16", [P, P], F16)
        epsln, epsrms = sb("epsln", [P, CT], F32), sb("epsrms", [P, CT], F32)
        mhalf, mone = sb("mhalf", [P, CT], F32), sb("mone", [P, CT], F32)
        tri = sb("tri", [P, CT, NE, NE], F32)
        sel = sb("sel", [2 * NE, NE, P], F16)
        wf = sb("wf", [P, N, CT], F32)
        wr1, wr2 = sb("wr1", [P, N, CT], F32), sb("wr2", [P, N, CT], F32)
        wparts = sb("wparts", [P, N, CT, 3], BF16)

        xin = sb("xin", [P, CT, D], F32)
        adjin = sb("adjin", [P, CT, C], F32)
        h16 = sb("h16", [P, CT, C], F16)
        ht16 = sb("ht16", [P, CT, C], F16)
        wcur = sb("wcur", [P, CT, 3], BF16)
        xbn = sb("xbn", [P, CT, 6], F32)
        xmv = sb("xmv", [P, CT, 2], F32)
        xve, xrs, xnm, xnb = (sb(n, [P, CT], F32) for n in ("xve", "xrs", "xnm", "xnb"))
        xn = sb("xn", [P, CT, D], F32)
        xsh, xsl = sb("xsh", [P, CT, D], F16), sb("xsl", [P, CT, D], F16)
        xsum = sb("xsum", [P, CT, D], F32)
        xb = sb("xb", [P, CT, D], F32)
        deg, dmax, be = (sb(n, [P, CT], F32) for n in ("deg", "dmax", "be"))
        dsum, dclip, drec, dn, dna, dnb = (sb(n, [P, CT], F32) for n in ("dsum", "dclip", "drec", "dn", "dna", "dnb"))
        a1h, a1l = sb("a1h", [P, CT, D], F16), sb("a1l", [P, CT, D], F16)
        a2h, a2l = sb("a2h", [P, KD, C], F16), sb("a2l", [P, KD, C], F16)
        z = sb("z", [P, CT, DH], F32)
        r = sb("r", [P, CT, DH], F32)
        hbn = sb("hbn", [P, CT, 6], F32)
        hmv = sb("hmv", [P, CT, 2], F32)
        hve, hrs, hnm, hnb = (sb(n, [P, CT], F32) for n in ("hve", "hrs", "hnm", "hnb"))
        hn = sb("hn", [P, CT, DH], F32)
        hnth, hntl = sb("hnth", [P, CT, KH * P], F16), sb("hntl", [P, CT, KH * P], F16)
        vh, vl = sb("vh", [P, CT, D], F16), sb("vl", [P, CT, D], F16)
        uh, ul = sb("uh", [P, CT, D], F16), sb("ul", [P, CT, D], F16)
        x1 = sb("x1", [P, CT, D], F32)
        ybn = sb("ybn", [P, CT, 6], F32)
        ymv = sb("ymv", [P, CT, 2], F32)
        yve, yrs, ynm, ynb = (sb(n, [P, CT], F32) for n in ("yve", "yrs", "ynm", "ynb"))

        x1k = sb("x1k", [P, CT, D], F32)
        x2 = sb("x2", [P, CT, D], F32)
        x2o = sb("x2o", [P, CT, D], F32)
        xth, xtl = sb("xth", [P, KD, C], F16), sb("xtl", [P, KD, C], F16)
        spare = sb("spare", [P, 1], F32)
        lg = sb("lg", [P, CT, NE], F32)
        ldf, tie, beat = (sb(n, [P, CT, NE, NE], F32) for n in ("ldf", "tie", "beat"))
        rank, lsel, arg, th, wt, mask = (sb(n, [P, CT, NE], F32) for n in ("rank", "lsel", "arg", "th", "wt", "mask"))
        lsum = sb("lsum", [P, CT], F32)
        silu = sb("silu", [P, 4, 512], F32)
        m16 = sb("m16", [P, CT, 2 * NE], F16)
        mt16 = sb("mt16", [2 * NE, C], F16)
        comb = sb("comb", [P, KD, C], F32)
        cth, ctl = sb("cth", [P, KD, C], F16), sb("ctl", [P, KD, C], F16)
        y = sb("y", [P, CT, D], F32)
        ysq = sb("ysq", [P, D], F32)
        yms, yme, yrr = (sb(n, [P, CT], F32) for n in ("yms", "yme", "yrr"))
        yf = sb("yf", [P, CT, D], F32)
        outb = sb("outb", [P, CT, D], F32)

        wrow_in, a_in, b_in, c_in, vb_row = (sem(n) for n in ("wrow_in", "a_in", "b_in", "c_in", "vb_row"))
        tables, wp_dn, a_max, b_max, c_max = (sem(n) for n in ("tables", "wp_dn", "a_max", "b_max", "c_max"))
        table_set, a_abs, b_abs, c_abs, a_hi, b_hi, c_hi = (
            sem(n) for n in ("table_set", "a_abs", "b_abs", "c_abs", "a_hi", "b_hi", "c_hi"))
        own, a_mag, b_mag, c_mag = (sem(n) for n in ("own", "a_mag", "b_mag", "c_mag"))
        a_scale, b_scale, c_scale = (sem(n) for n in ("a_scale", "b_scale", "c_scale"))
        a_lo, b_lo, c_lo, vb_dn = (sem(n) for n in ("a_lo", "b_lo", "c_lo", "vb_dn"))
        bw_rdy = sem("bw_rdy")

        x_in, adj_in, out_st = sem("x_in"), sem("adj_in"), sem("out_st")
        ht_rdy, a3_rdy, hnt_rdy = sem("ht_rdy"), sem("a3_rdy"), sem("hnt_rdy")
        a1_rdy, a2_rdy, v_rdy, u_rdy, b3_rdy = (sem(n) for n in ("a1_rdy", "a2_rdy", "v_rdy", "u_rdy", "b3_rdy"))
        xt_rdy, o_rdy = sem("xt_rdy"), sem("o_rdy")
        d_rdy, lg_rdy, mt_rdy = sem("d_rdy"), sem("lg_rdy"), sem("mt_rdy")
        mb_rdy = sem("mb_rdy")
        e_rdy = sem("e_rdy")
        ht_cp, a1_hi, relu_dn, hn_dn, hnt_hi, u_hi, x2_dn, sq_dn, xn_dn = (
            sem(n) for n in ("ht_cp", "a1_hi", "relu_dn", "hn_dn", "hnt_hi", "u_hi", "x2_dn", "sq_dn", "xn_dn"))
        a2_hi, v_hi, xt_hi, ct_hi = (sem(n) for n in ("a2_hi", "v_hi", "xt_hi", "ct_hi"))
        xs_hi, th_dn, mt_cp, x1_kept = sem("xs_hi"), sem("th_dn"), sem("mt_cp"), sem("x1_kept")
        silu_dn = sem("silu_dn")
        h_made, xs_lo, xstat, lg_dn, arg_dn, mask_dn = (
            sem(n) for n in ("h_made", "xs_lo", "xstat", "lg_dn", "arg_dn", "mask_dn"))
        d_step = sem("d_step")
        r_step = sem("r_step")
        a1_lo, z_dn, hbn_dn, hstat, hnt_lo, u_lo, x1_dn, ybn_dn, xbn_dn, yf_dn = (
            sem(n) for n in ("a1_lo", "z_dn", "hbn_dn", "hstat", "hnt_lo", "u_lo", "x1_dn", "ybn_dn", "xbn_dn", "yf_dn"))
        ystat, be_max, be_dn = sem("ystat"), sem("be_max"), sem("be_dn")
        a2_lo, v_lo, xt_lo, ct_lo, y_dn = (sem(n) for n in ("a2_lo", "v_lo", "xt_lo", "ct_lo", "y_dn"))
        comb_st = sem("comb_st")
        xrs_st, yrs_st = sem("xrs_st"), sem("yrs_st")
        hrs_st = sem("hrs_st")
        rr_st = sem("rr_st")
        xs_sum, xb_dn = sem("xs_sum"), sem("xb_dn")
        w_cur, x2o_dn = sem("w_cur"), sem("x2o_dn")
        out_rdy = sem("out_rdy")

        def steps(eng, body):
            body(eng, 0, conv=True, ffn=False, late=False, prep=True)
            body(eng, 1, conv=True, ffn=True, late=False, prep=True)
            with eng.Fori(2, N - 1) as g:
                body(eng, g, conv=True, ffn=True, late=True, prep=True)
            body(eng, N - 1, conv=True, ffn=True, late=True, prep=False)
            body(eng, N, conv=False, ffn=True, late=True, prep=False)
            body(eng, N + 1, conv=False, ffn=False, late=True, prep=False)

        block = ctx.enter_context(nc.Block())


        @block.sync
        def _(sp):
            sp.dma_start(wf[:, :, :], wrow).then_inc(wrow_in, 16)
            sp.dma_start(xin[:, :, :], x[0].rearrange("(t p) d -> p t d", p=P)).then_inc(x_in, 16)
            sp.dma_start(adjin[:, :, :], adj[0].rearrange("(t p) e -> p t e", p=P)).then_inc(adj_in, 16)
            for dst, src in ((w1f[:, :, :], w1t.rearrange("(k p) h -> p k h", p=P)),
                             (b1b[:, :], b1.to_broadcast([P, DH]))):
                sp.dma_start(dst, src).then_inc(a_in, 16)
            for dst, src in ((gam[:, :], gamma), (bet[:, :], beta),
                             (w2f[:, :, :], w2t.rearrange("(k p) f -> p k f", p=P)),
                             (b2b[:, :], b2.to_broadcast([P, D]))):
                sp.dma_start(dst, src).then_inc(b_in, 16)
            for dst, src in (
                (ewf[:, :, :].rearrange("p k (e h) -> p k e h", e=NE), ew.rearrange("(k p) e h -> p k e h", p=P)),
                (owf[:, :, :], ow.rearrange("(k p) h -> p k h", p=P)),
                (rwf[:, :, :], rw.rearrange("(k p) e -> p k e", p=P)),
                (ebcol[:, :], eb), (obb[:, :], ob.to_broadcast([P, D])),
                (nwb[:, :], nw.to_broadcast([P, D])), (rbb[:, 0, :], rb.to_broadcast([P, NE])),
            ):
                sp.dma_start(dst, src).then_inc(c_in, 16)

            def body(sp, g, conv, ffn, late, prep):
                if prep:
                    sp.wait_ge(xs_sum, g + 1)
                    sp.dma_start(xin[:, :, :], x[g + 1].rearrange("(t p) d -> p t d", p=P)).then_inc(x_in, 16)
                    sp.wait_ge(h_made, g + 1)
                    sp.dma_start(adjin[:, :, :], adj[g + 1].rearrange("(t p) e -> p t e", p=P)).then_inc(adj_in, 16)
                if conv and not ffn:
                    sp.wait_ge(vb_dn, 1)
                    for part in range(3):
                        sp.dma_start(vbias[32 * part:32 * part + 1, :], vbparts[:, part, :]).then_inc(vb_row, 16)
                if late:
                    q = g - 2
                    for j in range(2):
                        sp.wait_ge(out_rdy, 2 * q + j + 1)
                        sp.dma_start(out[q].rearrange("(t p) d -> p t d", p=P)[:, CG * j:CG * j + CG, :],
                                     outb[:, CG * j:CG * j + CG, :]).then_inc(out_st, 16)
            steps(sp, body)
            sp.wait_ge(out_st, 32 * N)

        @block.gpsimd
        def _(gp):
            tt = nc.gpsimd.tensor_tensor
            nc.gpsimd.memset(epsln[:, :], EPS_LN).then_inc(tables, 1)
            nc.gpsimd.memset(mhalf[:, :], -0.5).then_inc(tables, 1)
            nc.gpsimd.memset(mone[:, :], -1.0).then_inc(tables, 1)
            nc.gpsimd.memset(ident16[:, :], 0.0).then_inc(tables, 1)
            nc.gpsimd.memset(ident[:, :], 0.0).then_inc(tables, 1)
            nc.gpsimd.memset(tri[:, :, :, :], 1.0).then_inc(tables, 1)
            nc.gpsimd.memset(epsrms[:, :], EPS_RMS).then_inc(tables, 1)
            nc.gpsimd.memset(mags[:, :], 0.0).then_inc(tables, 1)
            nc.gpsimd.memset(ones[:, :], 1.0).then_inc(tables, 1)
            nc.gpsimd.memset(sel[:, :, :], 0.0).then_inc(tables, 1)
            nc.gpsimd.memset(vbias[:, :], 0.0).then_inc(tables, 1)
            gp.wait_ge(tables, 11)
            for m in (ident16, ident):
                gp.affine_select(out=m[:, :], in_=m[:, :], compare_op=ALU.not_equal, fill=1.0, base=0,
                                 pattern=[[-1, P]], channel_multiplier=1).then_inc(tables, 1)
            gp.affine_select(out=tri[:, :, :, :], in_=tri[:, :, :, :], compare_op=ALU.is_gt, fill=0.0, base=0,
                             pattern=[[0, CT], [1, NE], [-1, NE]], channel_multiplier=0).then_inc(tables, 1)
            for i, part in enumerate((0, NE)):
                gp.wait_ge(tables, 14 + i)
                gp.affine_select(out=sel[:, :, :], in_=sel[:, :, :], compare_op=ALU.not_equal, fill=1.0, base=-part,
                                 pattern=[[-1, NE], [0, P]], channel_multiplier=1).then_inc(tables, 1)
            gp.wait_ge(wrow_in, 16)
            nc.gpsimd.tensor_copy(wparts[:, :, :, 0], wf[:, :, :]).then_inc(wp_dn, 1)
            gp.wait_ge(wp_dn, 1)
            tt(wr1[:, :, :], wf[:, :, :], wparts[:, :, :, 0], ALU.subtract).then_inc(wp_dn, 1)
            gp.wait_ge(wp_dn, 2)
            nc.gpsimd.tensor_copy(wparts[:, :, :, 1], wr1[:, :, :]).then_inc(wp_dn, 1)
            gp.wait_ge(wp_dn, 3)
            tt(wr2[:, :, :], wr1[:, :, :], wparts[:, :, :, 1], ALU.subtract).then_inc(wp_dn, 1)
            gp.wait_ge(wp_dn, 4)
            nc.gpsimd.tensor_copy(wparts[:, :, :, 2], wr2[:, :, :]).then_inc(wp_dn, 1)
            gp.wait_ge(wp_dn, 5)

            def largest(s_mag, cols, s_max):
                gp.wait_ge(s_mag, 1)
                nc.gpsimd.partition_all_reduce(pmax[:, cols], mags[:, cols], P, RMAX).then_inc(s_max, 1)

            def root(stat, mv, ve, rs, nm, nb, sem_st, g, per, k, s, stat_per, stat_k):
                gp.wait_ge(stat, stat_per * g + stat_k)
                tt(ve[:, s], mv[:, s, 1], epsln[:, s], ALU.add).then_inc(sem_st, 1)
                tt(nm[:, s], mv[:, s, 0], mone[:, s], ALU.mult).then_inc(sem_st, 1)
                gp.wait_ge(sem_st, per * g + k + 2)
                tt(rs[:, s], ve[:, s], mhalf[:, s], ALU.pow).then_inc(sem_st, 1)
                gp.wait_ge(sem_st, per * g + k + 3)
                tt(nb[:, s], nm[:, s], rs[:, s], ALU.mult).then_inc(sem_st, 1)

            ALL = slice(0, CT)

            def prep_x(g, again=True):
                if again:
                    gp.wait_ge(d_rdy, g)
                root(xstat, xmv, xve, xrs, xnm, xnb, xrs_st, g, 4, 0, ALL, 1, 1)
                nc.gpsimd.tensor_copy(wcur[:, :, :], wparts[:, g, :, :]).then_inc(w_cur, 1)

            def sum_x(g, again=True):
                gp.wait_ge(xn_dn, 4 * g + 4)
                if again:
                    gp.wait_ge(xb_dn, g)
                tt(xsum[:, :, :], xin[:, :, :], xn[:, :, :], ALU.add).then_inc(xs_sum, 1)

            def make_xb(g, again=True):
                if again:
                    gp.wait_ge(x1_dn, 4 * g)
                gp.wait_ge(xs_sum, g + 1)
                tt(xb[:, :, :], xsum[:, :, :], b2b[:, :].unsqueeze(1).to_broadcast([P, CT, D]), ALU.add).then_inc(xb_dn, 1)

            prep_x(0, again=False)
            sum_x(0, again=False)
            largest(a_mag, slice(W1, W1 + 1), a_max)
            gp.wait_ge(b_in, 64)
            make_xb(0, again=False)

            def body(gp, g, conv, ffn, late, prep):
                f, q = g - 1, g - 2
                if late and ffn:
                    for j in range(2):
                        s = slice(CG * j, CG * j + CG)
                        gp.wait_ge(yf_dn, 4 * q + CG * j + CG)
                        tt(outb[:, s, :], yf[:, s, :], x1k[:, s, :], ALU.add).then_inc(out_rdy, 1)
                if conv and not ffn:
                    largest(b_mag, slice(W2, VB + 1), b_max)
                if prep and ffn:
                    prep_x(g + 1)
                if ffn:
                    gp.wait_ge(x2_dn, 4 * f + 4)
                    tt(x2o[:, :, :], x2[:, :, :], obb[:, :].unsqueeze(1).to_broadcast([P, CT, D]), ALU.add).then_inc(x2o_dn, 1)
                if prep and ffn:
                    sum_x(g + 1)
                if conv:
                    for t in range(CT):
                        root(hstat, hmv, hve, hrs, hnm, hnb, hrs_st, g, 16, 4 * t, slice(t, t + 1), 4, t + 1)
                if conv and not ffn:
                    prep_x(g + 1)
                    largest(c_mag, slice(EX, RW + 1), c_max)
                    sum_x(g + 1)
                if ffn:
                    if late:
                        gp.wait_ge(out_st, 32 * q + 32)
                    for j in range(1 if conv else 2):
                        s = ALL if conv else slice(CG * j, CG * j + CG)
                        gp.wait_ge(sq_dn, 4 * f + s.stop)
                        tt(yme[:, s], yms[:, s], epsrms[:, s], ALU.add).then_inc(rr_st, 1)
                        gp.wait_ge(rr_st, 2 * f + 2 * j + 1)
                        tt(yrr[:, s], yme[:, s], mhalf[:, s], ALU.pow).then_inc(rr_st, 1)
                if conv:
                    for j in range(2):
                        root(ystat, ymv, yve, yrs, ynm, ynb, yrs_st, g, 8, 4 * j, slice(CG * j, CG * j + CG), 2, j + 1)
                if prep:
                    make_xb(g + 1)
            steps(gp, body)

        @block.scalar
        def _(act):
            af = nc.scalar.activation

            def prep_x(g, tiles, again=True):
                if tiles[0] == 0:
                    act.wait_ge(xrs_st, 4 * g + 4)
                    if again:
                        act.wait_ge(xs_sum, g)
                        act.wait_ge(xs_lo, g)
                for t in tiles:
                    af(xn[:, t, :], xin[:, t, :], ACT.Identity, bias=xnb[:, t:t + 1],
                       scale=xrs[:, t:t + 1]).then_inc(xn_dn, 1)

            def prep_x_hi(g, again=True):
                act.wait_ge(xn_dn, 4 * g + 4)
                if again:
                    act.wait_ge(a1_rdy, 2 * g)
                af(xsh[:, :, :], xn[:, :, :], ACT.Copy, scale=XS).then_inc(xs_hi, 1)

            act.wait_ge(tables, 1)
            af(ysq[:, 0:1], epsln[:, 0:1], ACT.Silu).then_inc(table_set, 1)
            prep_x(0, range(CT), again=False)
            prep_x_hi(0, again=False)

            def flat3(t):
                return t[:, :, :].rearrange("p k n -> p (k n)")

            def setup_abs_a():
                act.wait_ge(a_in, 32)
                af(absbuf[:, 0, :], flat3(w1f), ACT.Abs).then_inc(a_abs, 1)

            def setup_abs_b():
                act.wait_ge(b_in, 64)
                for k in range(KH):
                    af(w2g[:, k, :], w2f[:, k, :], ACT.Copy, scale=gam[:, k:k + 1]).then_inc(b_abs, 1)
                act.wait_ge(b_abs, KH)
                af(absbuf[:, 1, :], flat3(w2g), ACT.Abs).then_inc(b_abs, 1)

            def setup_abs_ew():
                act.wait_ge(c_in, 16 * 7)
                af(silu[:, :, :].rearrange("p k n -> p (k n)"), flat3(ewf), ACT.Abs).then_inc(c_abs, 1)

            def setup_abs_c():
                af(x2[:, 0:2, :], owf[:, :, :], ACT.Abs).then_inc(c_abs, 1)
                af(x2[:, 2, 0:KD * NE], flat3(rwf), ACT.Abs).then_inc(c_abs, 1)

            def setup_hi(s_scale, parts, s_hi):
                act.wait_ge(s_scale, 1)
                for full, hi, col in parts:
                    af(hi[:, :, :], full[:, :, :], ACT.Copy, scale=wsc[:, col:col + 1]).then_inc(s_hi, 1)

            def expert(act, f, i):
                act.wait_ge(e_rdy, 8 * f + i + 1)
                if i >= 4:
                    act.wait_ge(comb_st, 7 * f + (1 if i < 6 else 3))
                af(silu[:, i % 4, :], bank[E_BANK[i]][:, :], ACT.Silu, bias=ebcol[:, i:i + 1],
                   scale=ksc[:, 2:3]).then_inc(silu_dn, 1)

            def mask_copy(act, f):
                act.wait_ge(mt_rdy, f + 1)
                af(mt16[:, :], bank[MT_BANK][0:2 * NE, 0:256].bitcast(F16), ACT.Copy).then_inc(mt_cp, 1)

            def relu(act, g, t):
                act.wait_ge(z_dn, 4 * g + t + 1)
                af(r[:, t, :], z[:, t, :], ACT.Relu).then_inc(relu_dn, 1)

            def norm_h(act, g, t):
                act.wait_ge(hrs_st, 16 * g + 4 * t + 4)
                af(hn[:, t, :], r[:, t, :], ACT.Identity, bias=hnb[:, t:t + 1],
                   scale=hrs[:, t:t + 1]).then_inc(hn_dn, 1)

            def hnt_part(act, g, t):
                act.wait_ge(hnt_rdy, 4 * g + t + 1)
                af(hnth[:, t, :], bank[HNT_BANK[t]][:, :], ACT.Copy, scale=HS).then_inc(hnt_hi, 1)

            def v_part(act, g, j):
                act.wait_ge(v_rdy, 2 * g + j + 1)
                af(vh[:, CG * j:CG * j + CG, :], bank[V_BANK[j]][:, :].rearrange("p (t d) -> p t d", t=CG),
                   ACT.Copy, scale=VS).then_inc(v_hi, 1)

            def ct_part(act, f, j):
                act.wait_ge(comb_st, 7 * f + 7)
                s = slice(256 * j, 256 * j + 256)
                af(cth[:, :, s], comb[:, :, s], ACT.Copy, scale=ksc[:, 5:6]).then_inc(ct_hi, 1)

            def squares(act, f, j):
                act.wait_ge(y_dn, 2 * f + j + 1)
                for t in range(CG * j, CG * j + CG):
                    if t > 0:
                        act.wait_ge(sq_dn, 4 * f + t)
                    af(ysq[:, :], y[:, t, :], ACT.Square, scale=D ** -0.5, accum_out=yms[:, t:t + 1]).then_inc(sq_dn, 1)

            def a1_part(act, g, j):
                act.wait_ge(be_dn, 2 * g + j + 1)
                act.wait_ge(a1_rdy, 2 * g + j + 1)
                for e in range(CG * j, CG * j + CG):
                    af(a1h[:, e, :], bank[A1_BANK[j]][:, D * (e % CG):D * (e % CG) + D], ACT.Copy,
                       scale=be[:, e:e + 1]).then_inc(a1_hi, 1)

            def x2_part(act, f, j):
                act.wait_ge(yrs_st, 8 * f + 4 * j + 4)
                for t in range(CG * j, CG * j + CG):
                    af(x2[:, t, :], x1[:, t, :], ACT.Identity, bias=ynb[:, t:t + 1],
                       scale=yrs[:, t:t + 1]).then_inc(x2_dn, 1)

            def body(act, g, conv, ffn, late, prep):
                f = g - 1
                if conv:
                    if ffn:
                        act.wait_ge(be_max, 2 * g)
                    for k in range(CT):
                        act.wait_ge(ht_rdy, 4 * g + k + 1)
                        af(ht16[:, k, :], bank[HT_BANK[k]][:, 0:256].bitcast(F16), ACT.Copy,
                           accum_out=deg[:, k:k + 1]).then_inc(ht_cp, 1)
                    if not ffn:
                        setup_abs_a()
                    a1_part(act, g, 0)
                    if not ffn:
                        setup_hi(a_scale, ((w1f, w1h, W1),), a_hi)
                if ffn:
                    x2_part(act, f, 0)
                if conv:
                    a1_part(act, g, 1)
                if conv and not ffn:
                    setup_abs_b()
                if ffn:
                    x2_part(act, f, 1)
                if conv and ffn and not late:
                    setup_hi(c_scale, ((ewf, ewh, EX),), c_hi)
                if ffn:
                    for j in range(2):
                        act.wait_ge(xt_rdy, 2 * f + j + 1)
                        af(xth[:, :, 256 * j:256 * j + 256],
                           bank[XT_BANK[j]][:, :].rearrange("p (k c) -> p k c", k=KD),
                           ACT.Copy, scale=XS).then_inc(xt_hi, 1)
                if conv:
                    for k in range(KD):
                        act.wait_ge(a2_rdy, 2 * g + k + 1)
                        af(a2h[:, k, :], bank[A2_BANK[k]][:, :], ACT.Copy, scale=A2S).then_inc(a2_hi, 1)
                if ffn:
                    expert(act, f, 0)
                if prep and ffn:
                    prep_x(g + 1, (0, 1))
                if ffn:
                    act.wait_ge(arg_dn, f + 1)
                    af(th[:, :, :], arg[:, :, :], ACT.Tanh).then_inc(th_dn, 1)
                    expert(act, f, 1)
                if prep and ffn:
                    prep_x(g + 1, (2, 3))
                if conv:
                    relu(act, g, 0)
                    relu(act, g, 1)
                if prep and ffn:
                    prep_x_hi(g + 1)
                if ffn:
                    mask_copy(act, f)
                if conv and not ffn:
                    norm_h(act, g, 0)
                    setup_hi(b_scale, ((w2g, w2h, W2),), b_hi)
                if conv:
                    relu(act, g, 2)
                if ffn:
                    expert(act, f, 2)
                if conv:
                    if ffn:
                        norm_h(act, g, 0)
                    relu(act, g, 3)
                if ffn:
                    expert(act, f, 3)
                if conv:
                    norm_h(act, g, 1)
                if ffn:
                    expert(act, f, 4)
                if conv:
                    if not ffn:
                        hnt_part(act, g, 0)
                    norm_h(act, g, 2)
                if ffn:
                    expert(act, f, 5)
                if conv:
                    if ffn:
                        hnt_part(act, g, 0)
                    else:
                        hnt_part(act, g, 1)
                        setup_abs_ew()
                    norm_h(act, g, 3)
                if conv:
                    if ffn:
                        hnt_part(act, g, 1)
                if ffn:
                    expert(act, f, 6)
                    expert(act, f, 7)
                if conv:
                    hnt_part(act, g, 2)
                    hnt_part(act, g, 3)
                    v_part(act, g, 0)
                if ffn:
                    ct_part(act, f, 0)
                    ct_part(act, f, 1)
                if conv:
                    v_part(act, g, 1)
                if ffn:
                    if late and not prep:
                        act.wait_ge(out_rdy, 2 * f)
                    af(x1k[:, :, :], x1[:, :, :], ACT.Copy).then_inc(x1_kept, 1)
                if conv and not ffn:
                    setup_abs_c()
                if conv:
                    for e in range(CT):
                        if e % CG == 0:
                            act.wait_ge(u_rdy, 2 * g + e // CG + 1)
                        af(uh[:, e, :], bank[U_BANK[e // CG]][:, D * (e % CG):D * (e % CG) + D], ACT.Copy,
                           scale=be[:, e:e + 1]).then_inc(u_hi, 1)
                if conv and not ffn:
                    prep_x(g + 1, range(CT))
                    prep_x_hi(g + 1)
                    setup_hi(c_scale, ((rwf, rwh, RW), (owf, owh, OW)), c_hi)
                if ffn:
                    squares(act, f, 0)
                    squares(act, f, 1)
            steps(act, body)

        @block.vector
        def _(dve):
            v = nc.vector
            TT, TS, STT = v.tensor_tensor, v.tensor_scalar, v.scalar_tensor_tensor
            count = [0]

            def done(ins):
                count[0] += 1
                ins.then_inc(own, 1)
                dve.wait_ge(own, count[0])

            def flat(t):
                return t[:, :, :, :].rearrange("p t e j -> p (t e j)")

            def prep_h(g, again=True):
                dve.wait_ge(adj_in, 16 * g + 16)
                if again:
                    dve.wait_ge(u_rdy, 2 * g)
                TS(h16[:, :, :], adjin[:, :, :], 0.0, None, ALU.not_equal).then_inc(h_made, 1)

            def prep_x_stats(g):
                dve.wait_ge(x_in, 16 * g + 16)
                for t in range(CT):
                    v.bn_stats(xbn[:, t, :], xin[:, t, :]).then_inc(xbn_dn, 1)

            def prep_x_aggr(g, again=True):
                dve.wait_ge(xbn_dn, 4 * g + 4)
                if again:
                    dve.wait_ge(xrs_st, 4 * g)
                v.memset(spare[:, :], 0.0)
                for t in range(CT):
                    ins = v.bn_aggr(xmv[:, t, :], xbn[:, t, :])
                ins.then_inc(xstat, 1)

            def prep_x_lo(g):
                dve.wait_ge(xs_hi, g + 1)
                STT(xsl[:, :, :], xn[:, :, :], XS, xsh[:, :, :], ALU.mult, ALU.subtract).then_inc(xs_lo, 1)

            prep_x_stats(0)
            prep_x_aggr(0, again=False)
            prep_h(0, again=False)
            prep_x_lo(0)

            def setup_scales(cols, paired):
                c0 = cols.start
                if paired:
                    done(TT(pmax[:, c0:c0 + 1], pmax[:, c0:c0 + 1], pmax[:, c0 + 1:c0 + 2], ALU.max))
                done(TS(pmax[:, cols], pmax[:, cols], 1e-30, 1e30, ALU.max, ALU.min))
                done(TS(pw[:, cols].bitcast(I32), pmax[:, cols].bitcast(I32), 0x7F800000, None, ALU.bitwise_and))
                done(v.reciprocal(ipw[:, cols], pw[:, cols]))
                done(TS(wsc[:, cols], ipw[:, cols], WS, None, ALU.mult))

            def setup_lo(s_hi, n, parts, s_lo):
                dve.wait_ge(s_hi, n)
                for full, hi, lo, col in parts:
                    STT(lo[:, :, :], full[:, :, :], wsc[:, col:col + 1], hi[:, :, :], ALU.mult,
                        ALU.subtract).then_inc(s_lo, 1)

            def setup_mag_a():
                dve.wait_ge(tables, 11)
                dve.wait_ge(a_abs, 1)
                v.reduce_max(mags[:, W1:W1 + 1], absbuf[:, 0, :], X).then_inc(a_mag, 1)

            def setup_scale_a():
                dve.wait_ge(a_max, 1)
                setup_scales(slice(W1, W1 + 1), False)
                v.tensor_scalar(ksc[:, 0:1], pw[:, W1:W1 + 1], 1.0 / (XS * A2S * WS), None, ALU.mult).then_inc(a_scale, 1)
                dve.wait_ge(a_scale, 1)

            def mag_small(src, n, cols, scale):
                done(STT(babs[:, 0:n], src[:, 0:n], -1.0, src[:, 0:n], ALU.mult, ALU.max))
                done(v.reduce_max(mags[:, cols:cols + 1], babs[:, 0:n], X))
                done(TS(mags[:, cols:cols + 1], mags[:, cols:cols + 1], scale, None, ALU.mult))

            def setup_mag_b():
                dve.wait_ge(bw_rdy, 1)
                done(v.tensor_copy(bwcol[:, :], bank[7][:, 0:D // P]))
                mag_small(bwcol, D // P, VB, 1.0 / DH)
                dve.wait_ge(b_abs, KH + 1)
                v.reduce_max(mags[:, W2:W2 + 1], absbuf[:, 1, :], X).then_inc(b_mag, 1)

            def setup_bias(src, n, col, scale, parts, s_dn):
                done(TS(bval[:, 0:n], src[:, :], wsc[:, col:col + 1], scale, ALU.mult, ALU.mult))
                for part in range(3):
                    ins = v.tensor_copy(parts[:, part, :], bval[:, 0:n])
                    if part < 2:
                        done(ins)
                        done(TT(bval[:, 0:n], bval[:, 0:n], parts[:, part, :], ALU.subtract))
                ins.then_inc(s_dn, 1)
                dve.wait_ge(s_dn, 1)

            def setup_scale_b():
                dve.wait_ge(b_max, 1)
                setup_scales(slice(W2, VB + 1), True)
                v.tensor_scalar(ksc[:, 1:2], pw[:, W2:W2 + 1], 1.0 / (HS * WS * VS), None, ALU.mult).then_inc(b_scale, 1)
                dve.wait_ge(b_scale, 1)

            def setup_mag_ew():
                dve.wait_ge(c_abs, 1)
                v.reduce_max(mags[:, EX:EX + 1], silu[:, :, :].rearrange("p k n -> p (k n)"), X)
                for t in range(1, CT):
                    v.tensor_copy(rbb[:, t, :], rbb[:, 0, :])
                mag_small(ebcol, NE * D // P, EB, 1.0 / D)

            def setup_mag_c():
                dve.wait_ge(c_abs, 3)
                v.reduce_max(mags[:, OW:OW + 1], x2[:, 0:2, :].rearrange("p k n -> p (k n)"), X)
                v.reduce_max(mags[:, RW:RW + 1], x2[:, 2, 0:KD * NE], X).then_inc(c_mag, 1)

            def setup_scale_c():
                dve.wait_ge(c_max, 1)
                setup_scales(slice(EX, RW + 1), True)
                TS(ksc[:, 2:3], pw[:, EX:EX + 1], 1.0 / (XS * WS), None, ALU.mult)
                TS(ksc[:, 3:4], pw[:, OW:OW + 1], 2.0 ** -5 / WS, pw[:, EX:EX + 1], ALU.mult, ALU.mult)
                TS(ksc[:, 4:5], pw[:, RW:RW + 1], 1.0 / (XS * WS), None, ALU.mult)
                TS(ksc[:, 5:6], ipw[:, EX:EX + 1], 2.0 ** 5, None, ALU.mult).then_inc(c_scale, 1)
                dve.wait_ge(c_scale, 1)

            def combine(f, e):
                src = silu[:, 2 * (e % 2):2 * (e % 2) + 2, :]
                m = bank[MB_BANK[e]][:, :].unsqueeze(1).to_broadcast([P, KD, C])
                dve.wait_ge(mb_rdy, 4 * f + e + 1)
                dve.wait_ge(silu_dn, 8 * f + 2 * e + 2)
                if e == 0:
                    TT(comb[:, :, :], src, m, ALU.mult).then_inc(comb_st, 1)
                else:
                    TT(src, src, m, ALU.mult).then_inc(comb_st, 1)

            def combine_sum(f, e):
                dve.wait_ge(comb_st, 7 * f + 2 * e)
                TT(comb[:, :, :], comb[:, :, :], silu[:, 2 * (e % 2):2 * (e % 2) + 2, :], ALU.add).then_inc(comb_st, 1)

            def z_part(g, t):
                dve.wait_ge(a3_rdy, 4 * g + t + 1)
                STT(z[:, t, :], bank[A3_BANK[t]][:, :], dna[:, t:t + 1], b1b[:, :], ALU.mult, ALU.add).then_inc(z_dn, 1)

            def h_stats(g, t):
                dve.wait_ge(relu_dn, 4 * g + t + 1)
                v.bn_stats(hbn[:, t, :], r[:, t, :]).then_inc(hbn_dn, 1)

            def h_aggr(g, t):
                v.bn_aggr(hmv[:, t, :], hbn[:, t, :]).then_inc(hstat, 1)

            def hnt_part(g, t):
                dve.wait_ge(hnt_hi, 4 * g + t + 1)
                STT(hntl[:, t, :], bank[HNT_BANK[t]][:, :], HS, hnth[:, t, :], ALU.mult, ALU.subtract).then_inc(hnt_lo, 1)

            def v_part(g, j):
                dve.wait_ge(v_hi, 2 * g + j + 1)
                s = slice(CG * j, CG * j + CG)
                STT(vl[:, s, :], bank[V_BANK[j]][:, :].rearrange("p (t d) -> p t d", t=CG), VS, vh[:, s, :],
                    ALU.mult, ALU.subtract).then_inc(v_lo, 1)

            def ct_part(f, j):
                dve.wait_ge(ct_hi, 2 * f + j + 1)
                s = slice(256 * j, 256 * j + 256)
                STT(ctl[:, :, s], comb[:, :, s], ksc[:, 5:6], cth[:, :, s], ALU.mult, ALU.subtract).then_inc(ct_lo, 1)

            def y_part(f, j):
                dve.wait_ge(o_rdy, 2 * f + j + 1)
                if j == 0:
                    dve.wait_ge(x2o_dn, f + 1)
                s = slice(CG * j, CG * j + CG)
                STT(y[:, s, :], bank[O_BANK[j]][:, :].rearrange("p (t d) -> p t d", t=CG), ksc[:, 3:4], x2o[:, s, :],
                    ALU.mult, ALU.add).then_inc(y_dn, 1)

            def a1_part(g, j):
                dve.wait_ge(a1_hi, 4 * g + CG * j + CG)
                for e in range(CG * j, CG * j + CG):
                    STT(a1l[:, e, :], bank[A1_BANK[j]][:, D * (e % CG):D * (e % CG) + D], be[:, e:e + 1], a1h[:, e, :],
                        ALU.mult, ALU.subtract).then_inc(a1_lo, 1)

            def d_vector(g):
                dve.wait_ge(d_rdy, g + 1)
                v.reduce_sum(dsum[:, :], bank[D_BANK][:, 0:CT * 4].rearrange("p (t w) -> p t w", w=4)[:, :, 0:3],
                             X).then_inc(d_step, 1)
                dve.wait_ge(d_step, 6 * g + 1)
                TS(dclip[:, :], dsum[:, :], 1.2e-38, None, ALU.max).then_inc(d_step, 1)
                dve.wait_ge(d_step, 6 * g + 2)
                v.reciprocal(drec[:, :], dclip[:, :]).then_inc(d_step, 1)
                dve.wait_ge(d_step, 6 * g + 3)
                STT(dn[:, :], dsum[:, :], 0.0, drec[:, :], ALU.is_gt, ALU.mult).then_inc(d_step, 1)
                dve.wait_ge(d_step, 6 * g + 4)
                TS(dna[:, :], dn[:, :], ksc[:, 0:1], None, ALU.mult).then_inc(d_step, 1)

            def route(f):
                dve.wait_ge(lg_rdy, f + 1)
                STT(lg[:, :, :], bank[R_BANK][:, 0:CT * NE].rearrange("p (t e) -> p t e", e=NE), ksc[:, 4:5],
                    rbb[:, :, :], ALU.mult, ALU.add).then_inc(lg_dn, 1)
                dve.wait_ge(lg_dn, f + 1)
                TT(ldf[:, :, :, :], lg[:, :, :].unsqueeze(2).to_broadcast([P, CT, NE, NE]),
                   lg[:, :, :].unsqueeze(3).to_broadcast([P, CT, NE, NE]), ALU.subtract).then_inc(r_step, 1)
                dve.wait_ge(r_step, 9 * f + 1)
                STT(flat(tie), flat(ldf), 0.0, flat(tri), ALU.is_ge, ALU.mult).then_inc(r_step, 1)
                dve.wait_ge(r_step, 9 * f + 2)
                STT(flat(beat), flat(ldf), 0.0, flat(tie), ALU.is_gt, ALU.max).then_inc(r_step, 1)
                dve.wait_ge(r_step, 9 * f + 3)
                v.reduce_sum(rank[:, :, :], beat[:, :, :, :], X).then_inc(r_step, 1)
                dve.wait_ge(r_step, 9 * f + 4)
                STT(lsel[:, :, :], rank[:, :, :], 1.5, lg[:, :, :], ALU.is_lt, ALU.mult).then_inc(r_step, 1)
                dve.wait_ge(r_step, 9 * f + 5)
                v.reduce_sum(lsum[:, :], lsel[:, :, :], X).then_inc(r_step, 1)
                dve.wait_ge(r_step, 9 * f + 6)
                STT(arg[:, :, :], lsum[:, :].unsqueeze(2).to_broadcast([P, CT, NE]), -0.5, lg[:, :, :],
                    ALU.mult, ALU.add).then_inc(arg_dn, 1)

            def make_mask(f):
                dve.wait_ge(th_dn, f + 1)
                TS(wt[:, :, :], th[:, :, :], 0.5, 0.5, ALU.mult, ALU.add).then_inc(r_step, 1)
                dve.wait_ge(r_step, 9 * f + 7)
                STT(mask[:, :, :], rank[:, :, :], 1.5, wt[:, :, :], ALU.is_lt, ALU.mult).then_inc(r_step, 1)
                dve.wait_ge(r_step, 9 * f + 8)
                v.tensor_copy(m16[:, :, 0:NE], mask[:, :, :]).then_inc(r_step, 1)
                dve.wait_ge(r_step, 9 * f + 9)
                TT(m16[:, :, NE:2 * NE], mask[:, :, :], m16[:, :, 0:NE], ALU.subtract).then_inc(mask_dn, 1)

            def finish(q, tiles, last):
                for t in tiles:
                    dve.wait_ge(rr_st, 2 * q + (4 if last and t >= CG else 2))
                    STT(yf[:, t, :], y[:, t, :], yrr[:, t:t + 1], nwb[:, :], ALU.mult, ALU.mult).then_inc(yf_dn, 1)

            def add_out(q, j):
                dve.wait_ge(yf_dn, 4 * q + CG * j + CG)
                s = slice(CG * j, CG * j + CG)
                TT(outb[:, s, :], yf[:, s, :], x1k[:, s, :], ALU.add).then_inc(out_rdy, 1)

            def x1_half(g, j, again):
                if j == 0:
                    dve.wait_ge(xb_dn, g + 1)
                    dve.wait_ge(d_step, 6 * g + 6)
                    if again:
                        dve.wait_ge(x1_kept, g)
                dve.wait_ge(b3_rdy, 2 * g + j + 1)
                for t in range(CG * j, CG * j + CG):
                    STT(x1[:, t, :], bank[B3_BANK[j]][:, D * (t % CG):D * (t % CG) + D],
                        dnb[:, t:t + 1], xb[:, t, :], ALU.mult, ALU.add).then_inc(x1_dn, 1)

            def stats_x1(g, j):
                for t in range(CG * j, CG * j + CG):
                    dve.wait_ge(x1_dn, 4 * g + t + 1)
                    v.bn_stats(ybn[:, t, :], x1[:, t, :]).then_inc(ybn_dn, 1)
                dve.wait_ge(ybn_dn, 4 * g + CG * j + CG)
                v.memset(spare[:, :], 0.0)
                for t in range(CG * j, CG * j + CG):
                    ins = v.bn_aggr(ymv[:, t, :], ybn[:, t, :])
                ins.then_inc(ystat, 1)

            def degrees(g, j):
                s = slice(CG * j, CG * j + CG)
                dve.wait_ge(ht_cp, 4 * g + CG * j + CG)
                TS(dmax[:, s], deg[:, s], 1.0, None, ALU.max).then_inc(be_max, 1)
                dve.wait_ge(be_max, 2 * g + j + 1)
                v.reciprocal(be[:, s], dmax[:, s]).then_inc(be_dn, 1)

            def body(dve, g, conv, ffn, late, prep):
                f, q = g - 1, g - 2
                if ffn:
                    x1_half(f, 0, late)
                    stats_x1(f, 0)
                    x1_half(f, 1, late)
                if conv:
                    degrees(g, 0)
                if ffn:
                    stats_x1(f, 1)
                if conv:
                    degrees(g, 1)
                    if not ffn:
                        setup_mag_a()
                        setup_scale_a()
                if conv and ffn and not late:
                    setup_lo(c_hi, 2, ((rwf, rwh, rwl, RW), (owf, owh, owl, OW)), c_lo)
                if late:
                    finish(q, (0, 1), not ffn)
                if late and not ffn:
                    add_out(q, 0)
                if conv:
                    a1_part(g, 0)
                if late:
                    finish(q, (2, 3), not ffn)
                if late and not ffn:
                    add_out(q, 1)
                if conv:
                    a1_part(g, 1)
                if conv and not ffn:
                    setup_lo(a_hi, 1, ((w1f, w1h, w1l, W1),), a_lo)
                if prep and ffn:
                    prep_x_stats(g + 1)
                if ffn:
                    for j in range(2):
                        dve.wait_ge(xt_hi, 2 * f + j + 1)
                        s = slice(256 * j, 256 * j + 256)
                        STT(xtl[:, :, s], bank[XT_BANK[j]][:, :].rearrange("p (k c) -> p k c", k=KD), XS,
                            xth[:, :, s], ALU.mult, ALU.subtract).then_inc(xt_lo, 1)
                if conv and ffn and not late:
                    setup_lo(c_hi, 3, ((ewf, ewh, ewl, EX),), c_lo)
                if conv:
                    d_vector(g)
                if prep and ffn:
                    prep_x_aggr(g + 1)
                if conv:
                    dve.wait_ge(a2_hi, 2 * g + 1)
                    STT(a2l[:, 0, :], bank[A2_BANK[0]][:, :], A2S, a2h[:, 0, :], ALU.mult,
                        ALU.subtract).then_inc(a2_lo, 1)
                    dve.wait_ge(a2_hi, 2 * g + 2)
                    STT(a2l[:, 1, :], bank[A2_BANK[1]][:, :], A2S, a2h[:, 1, :], ALU.mult,
                        ALU.subtract).then_inc(a2_lo, 1)
                if ffn:
                    route(f)
                    make_mask(f)
                if conv:
                    if not ffn:
                        setup_mag_b()
                    dve.wait_ge(d_step, 6 * g + 5)
                    z_part(g, 0)
                if conv:
                    z_part(g, 1)
                if conv:
                    h_stats(g, 0)
                    dve.wait_ge(hbn_dn, 4 * g + 1)
                    if not ffn:
                        v.memset(spare[:, :], 0.0)
                        h_aggr(g, 0)
                        setup_scale_b()
                        setup_bias(bwcol, D // P, W2, HS, vbparts, vb_dn)
                    z_part(g, 2)
                    if ffn:
                        h_aggr(g, 0)
                    h_stats(g, 1)
                    dve.wait_ge(hbn_dn, 4 * g + 2)
                    z_part(g, 3)
                    h_aggr(g, 1)
                    TS(dnb[:, :], dn[:, :], ksc[:, 1:2], None, ALU.mult).then_inc(d_step, 1)
                    h_stats(g, 2)
                if ffn:
                    combine(f, 0)
                if conv:
                    dve.wait_ge(hbn_dn, 4 * g + 3)
                    v.memset(spare[:, :], 0.0)
                    h_aggr(g, 2)
                    if not ffn:
                        setup_lo(b_hi, 1, ((w2g, w2h, w2l, W2),), b_lo)
                        hnt_part(g, 0)
                    h_stats(g, 3)
                    dve.wait_ge(hbn_dn, 4 * g + 4)
                    v.memset(spare[:, :], 0.0)
                    h_aggr(g, 3)
                if ffn:
                    combine(f, 1)
                    combine_sum(f, 1)
                if conv and ffn:
                    hnt_part(g, 0)
                if ffn:
                    combine(f, 2)
                if conv:
                    hnt_part(g, 1)
                    if not ffn:
                        setup_mag_ew()
                if ffn:
                    combine_sum(f, 2)
                    combine(f, 3)
                if conv:
                    hnt_part(g, 2)
                if ffn:
                    combine_sum(f, 3)
                if conv:
                    hnt_part(g, 3)
                    v_part(g, 0)
                    if not ffn:
                        prep_x_stats(g + 1)
                        prep_x_aggr(g + 1)
                if ffn:
                    ct_part(f, 0)
                    ct_part(f, 1)
                if conv:
                    v_part(g, 1)
                if prep and ffn:
                    prep_x_lo(g + 1)
                if ffn:
                    y_part(f, 0)
                if conv and not ffn:
                    setup_mag_c()
                if conv:
                    for e in range(CT):
                        if e % CG == 0:
                            dve.wait_ge(u_hi, 4 * g + e + CG)
                        STT(ul[:, e, :], bank[U_BANK[e // CG]][:, D * (e % CG):D * (e % CG) + D],
                            be[:, e:e + 1], uh[:, e, :], ALU.mult, ALU.subtract).then_inc(u_lo, 1)
                if ffn:
                    y_part(f, 1)
                if prep:
                    prep_h(g + 1)
                    if not ffn:
                        setup_scale_c()
                        prep_x_lo(g + 1)
            steps(dve, body)

        @block.tensor
        def _(pe):
            mm = nc.tensor.matmul

            def three(outp, lh, ll, rh, rl, first, last):
                mm(outp, lh, rh, start=first, stop=False)
                mm(outp, lh, rl, start=False, stop=False)
                return mm(outp, ll, rh, start=False, stop=last)

            def beta_w2():
                pe.wait_ge(b_in, 64)
                for m in range(D // P):
                    for k in range(KH):
                        ins = mm(bank[7][:, m:m + 1], w2f[:, k, :].rearrange("p (n m) -> p m n", m=D // P)[:, m, :], bet[:, k:k + 1],
                                 start=(k == 0), stop=(k == KH - 1))
                ins.then_inc(bw_rdy, 1)

            def expert_half(f, i):
                if i == 2:
                    pe.wait_ge(lg_dn, f + 1)
                if i >= 3:
                    pe.wait_ge(silu_dn, 8 * f + i - 2)
                for k in range(KD):
                    ins = three(bank[E_BANK[i]][:, :], ewh[:, k, P * i:P * i + P], ewl[:, k, P * i:P * i + P],
                                xth[:, k, :], xtl[:, k, :], k == 0, k == KD - 1)
                ins.then_inc(e_rdy, 1)

            def transposed_mask(f):
                pe.wait_ge(mask_dn, f + 1)
                for t in range(CT):
                    ins = nc.tensor.transpose(bank[MT_BANK][0:2 * NE, 0:256].bitcast(F16)[:, P * t:P * t + P],
                                              m16[:, t, :], ident16[:, :])
                ins.then_inc(mt_rdy, 1)

            def mask_rows(f, e, g, conv):
                if e == 0:
                    pe.wait_ge(mt_cp, f + 1)
                if e < 2 and conv:
                    pe.wait_ge(z_dn, 4 * g + e + 2)
                if e >= 2:
                    pe.wait_ge(comb_st, 7 * f + e - 1)
                mm(bank[MB_BANK[e]][:, :], sel[:, e, :], mt16[:, :], start=True, stop=True).then_inc(mb_rdy, 1)

            def transposed_h(g, t):
                pe.wait_ge(hn_dn, 4 * g + t + 1)
                if t >= 2:
                    pe.wait_ge(hnt_lo, 4 * g + t - 1)
                for k in range(KH):
                    ins = nc.tensor.transpose(bank[HNT_BANK[t]][:, P * k:P * k + P], hn[:, t, P * k:P * k + P], ident[:, :])
                ins.then_inc(hnt_rdy, 1)

            def v_tile(g, t):
                pe.wait_ge(hnt_lo, 4 * g + t + 1)
                if t == 0:
                    pe.wait_ge(z_dn, 4 * g + 4)
                b = bank[V_BANK[t // CG]][:, D * (t % CG):D * (t % CG) + D]
                mm(b, ones[:, :], vbias[:, :], start=True, stop=False)
                for k in range(KH):
                    ins = three(b, hnth[:, t, P * k:P * k + P], hntl[:, t, P * k:P * k + P], w2h[:, k, :], w2l[:, k, :],
                                False, k == KH - 1)
                if t % CG == CG - 1:
                    ins.then_inc(v_rdy, 1)

            def out_product(f, j):
                pe.wait_ge(ct_lo, 2 * f + j + 1)
                for t in range(CG * j, CG * j + CG):
                    b = bank[O_BANK[j]][:, D * (t % CG):D * (t % CG) + D]
                    for k in range(KD):
                        ins = three(b, cth[:, k, P * t:P * t + P], ctl[:, k, P * t:P * t + P], owh[:, k, :], owl[:, k, :],
                                    k == 0, k == KD - 1)
                ins.then_inc(o_rdy, 1)

            def incidence(g, banks, weights, hi, lo, s_lo, per, s_rdy):
                def part(e, ks):
                    b = bank[banks[e // CG]][:, D * (e % CG):D * (e % CG) + D]
                    for k in ks:
                        mm(b, weights[:, k, P * e:P * e + P], hi[:, k, :], start=(k == 0), stop=False)
                        ins = mm(b, weights[:, k, P * e:P * e + P], lo[:, k, :], start=False, stop=(k == CT - 1))
                    return ins

                pe.wait_ge(s_lo, per * g + per // 2)
                part(0, (0, 1))
                part(CG, (0, 1))
                pe.wait_ge(s_lo, per * g + per)
                part(0, (2, 3))
                part(1, range(CT)).then_inc(s_rdy, 1)
                part(CG, (2, 3))
                part(CG + 1, range(CT)).then_inc(s_rdy, 1)

            def a2_half(g, half):
                pe.wait_ge(a1_lo, 4 * g + CG * half + CG)
                for d in range(KD):
                    if half == 0:
                        pe.wait_ge(ht_cp, 4 * g + 3 + d)
                    for k in range(CG * half, CG * half + CG):
                        mm(bank[A2_BANK[d]][:, :], a1h[:, k, P * d:P * d + P], ht16[:, k, :],
                           start=(k == 0), stop=False)
                        ins = mm(bank[A2_BANK[d]][:, :], a1l[:, k, P * d:P * d + P], ht16[:, k, :],
                                 start=False, stop=(k == CT - 1))
                    if half == 1:
                        ins.then_inc(a2_rdy, 1)

            def body(pe, g, conv, ffn, late, prep):
                f = g - 1
                if conv:
                    pe.wait_ge(h_made, g + 1)
                    for k in range(CT):
                        if ffn:
                            if k == 0:
                                pe.wait_ge(hnt_lo, 4 * g)
                            elif k == 1:
                                pe.wait_ge(u_lo, 4 * (g - 1) + 2)
                            elif k == 2:
                                pe.wait_ge(u_lo, 4 * g)
                            else:
                                pe.wait_ge(x1_dn, 4 * (g - 1) + 2)
                        for c in range(CT):
                            ins = nc.tensor.transpose(bank[HT_BANK[k]][:, 0:256].bitcast(F16)[:, P * c:P * c + P],
                                                      h16[:, c, P * k:P * k + P], ident16[:, :])
                        ins.then_inc(ht_rdy, 1)
                    pe.wait_ge(xs_lo, g + 1)
                    for e in range(CT):
                        if e % CG == 0:
                            pe.wait_ge(ht_cp, 4 * g + e // CG + 1)
                        b = bank[A1_BANK[e // CG]][:, D * (e % CG):D * (e % CG) + D]
                        for k in range(CT):
                            mm(b, h16[:, k, P * e:P * e + P], xsh[:, k, :], start=(k == 0), stop=False)
                            ins = mm(b, h16[:, k, P * e:P * e + P], xsl[:, k, :], start=False, stop=(k == CT - 1))
                        if e % CG == CG - 1:
                            ins.then_inc(a1_rdy, 1)
                    pe.wait_ge(ht_cp, 4 * g + 4)
                    pe.wait_ge(w_cur, g + 1)
                    if ffn:
                        pe.wait_ge(x1_dn, 4 * g)
                    for t in range(CT):
                        for k in range(CT):
                            ins = mm(bank[D_BANK][:, 4 * t:4 * t + 3], ht16[:, k, P * t:P * t + P], wcur[:, k, :],
                                     start=(k == 0), stop=(k == CT - 1))
                    ins.then_inc(d_rdy, 1)
                if conv:
                    a2_half(g, 0)
                if ffn:
                    for j in range(2):
                        pe.wait_ge(x2_dn, 4 * f + CG * j + CG)
                        for k in range(KD):
                            for t in range(CG):
                                ins = nc.tensor.transpose(bank[XT_BANK[j]][:, 256 * k + P * t:256 * k + P * t + P],
                                                          x2[:, CG * j + t, P * k:P * k + P], ident[:, :])
                        ins.then_inc(xt_rdy, 1)
                if conv:
                    a2_half(g, 1)
                if ffn:
                    if not late:
                        pe.wait_ge(c_lo, 2)
                    pe.wait_ge(xt_lo, 2 * f + 2)
                    for t in range(CT):
                        for k in range(KD):
                            ins = three(bank[R_BANK][:, NE * t:NE * t + NE], xth[:, k, P * t:P * t + P],
                                        xtl[:, k, P * t:P * t + P], rwh[:, k, :], rwl[:, k, :], k == 0, k == KD - 1)
                    ins.then_inc(lg_rdy, 1)
                    if not late:
                        pe.wait_ge(c_lo, 3)
                    expert_half(f, 0)
                    expert_half(f, 1)
                if conv:
                    if not ffn:
                        beta_w2()
                        pe.wait_ge(a_lo, 1)
                    pe.wait_ge(a2_lo, 2 * g + 2)
                    for t in range(CT):
                        for k in range(KD):
                            ins = three(bank[A3_BANK[t]][:, :], a2h[:, k, P * t:P * t + P], a2l[:, k, P * t:P * t + P],
                                        w1h[:, k, :], w1l[:, k, :], k == 0, k == KD - 1)
                        ins.then_inc(a3_rdy, 1)
                        if ffn and t == 2:
                            transposed_mask(f)
                elif ffn:
                    transposed_mask(f)
                if ffn:
                    expert_half(f, 2)
                    mask_rows(f, 0, g, conv)
                    expert_half(f, 3)
                    mask_rows(f, 1, g, conv)
                    expert_half(f, 4)
                    expert_half(f, 5)
                    mask_rows(f, 2, g, conv)
                if conv:
                    transposed_h(g, 0)
                    transposed_h(g, 1)
                if ffn:
                    expert_half(f, 6)
                    mask_rows(f, 3, g, conv)
                    expert_half(f, 7)
                if conv and not ffn:
                    pe.wait_ge(b_lo, 1)
                    pe.wait_ge(vb_row, 48)
                if conv:
                    v_tile(g, 0)
                    transposed_h(g, 2)
                    v_tile(g, 1)
                    transposed_h(g, 3)
                    v_tile(g, 2)
                if conv:
                    v_tile(g, 3)
                if ffn:
                    out_product(f, 0)
                if conv:
                    incidence(g, U_BANK, h16, vh, vl, v_lo, 2, u_rdy)
                if ffn:
                    out_product(f, 1)
                if conv:
                    incidence(g, B3_BANK, ht16, uh, ul, u_lo, 4, b3_rdy)

            pe.wait_ge(tables, 16)
            steps(pe, body)


def kernel(x, adj, L0_gnn_W1, L0_gnn_b1, L0_gnn_gamma, L0_gnn_beta, L0_gnn_W2, L0_gnn_b2, L0_ffn_router_w,
           L0_ffn_router_b, L0_ffn_expert_w, L0_ffn_expert_b, L0_ffn_out_w, L0_ffn_out_b, L0_ffn_norm_w):
    import numpy as np
    import concourse.bacc as bacc
    from concourse.bass_utils import run_bass_kernel_spmd

    def arr(a):
        return np.ascontiguousarray(a)

    x, adj = np.asarray(x), np.asarray(adj)
    n, c, d = x.shape
    dh = L0_gnn_b1.shape[0]
    ne = L0_ffn_expert_w.shape[0]
    arrays = {
        "x": arr(x),
        "adj": arr(adj),
        "wrow": arr(adj[:, 0, :].reshape(n, c // P, P).transpose(2, 0, 1)),
        "w1t": arr(np.asarray(L0_gnn_W1).T),
        "b1": arr(np.asarray(L0_gnn_b1).reshape(1, dh)),
        "gamma": arr(np.asarray(L0_gnn_gamma).reshape(dh // P, P).T),
        "beta": arr(np.asarray(L0_gnn_beta).reshape(dh // P, P).T),
        "w2t": arr(np.asarray(L0_gnn_W2).T),
        "b2": arr(np.asarray(L0_gnn_b2).reshape(1, d)),
        "rw": arr(L0_ffn_router_w),
        "rb": arr(np.asarray(L0_ffn_router_b).reshape(1, ne)),
        "ew": arr(np.asarray(L0_ffn_expert_w).transpose(1, 0, 2)),
        "eb": arr(np.asarray(L0_ffn_expert_b).reshape(ne * d // P, P).T),
        "ow": arr(L0_ffn_out_w),
        "ob": arr(np.asarray(L0_ffn_out_b).reshape(1, d)),
        "nw": arr(np.asarray(L0_ffn_norm_w).reshape(1, d)),
    }
    nc = bacc.Bacc("TRN2", target_bir_lowering=False, num_devices=1)
    args = [nc.dram_tensor(k, a.shape, mybir.dt.from_np(a.dtype), kind="ExternalInput").ap() for k, a in arrays.items()]
    res = nc.dram_tensor("out", (n, c, d), F32, kind="ExternalOutput").ap()
    build(nc, *args, res)
    got = run_bass_kernel_spmd(nc, [arrays], core_ids=[0])
    return got.results[0]["out"]
```
